# Optimizing a Trainium2 kernel written in Bass

```python
import numpy as np
import jax
import jax.numpy as jnp

def _softmax(x, axis=-1):
    return jax.nn.softmax(x, axis=axis)

def _gelu(x):
    return jax.nn.gelu(x, approximate=True)

def _silu(x):
    return jax.nn.silu(x)

def _sigmoid(x):
    return jax.nn.sigmoid(x)

def _layernorm(x, axis=-1, eps=1e-05):
    m = jnp.mean(x, axis=axis, keepdims=True)
    v = jnp.var(x, axis=axis, keepdims=True)
    return (x - m) / jnp.sqrt(v + eps)

def _scatter_add(tgt, idx, src, axis=0):
    return tgt.at[idx].add(src)

def _segment_sum(src, seg, n):
    return jax.ops.segment_sum(src, seg, n)
kernel_name = 'mk_hybrid_d1_jaxref_r4_16d077'

def setup_inputs(seed: int=0):
    np.random.seed(seed)
    _w = jnp.asarray

    def _L0_attn_a_setup():
        import jax, jax.numpy as jnp
        import numpy as np
        B, N, D, H = (2, 512, 512, 16)
        HD = D // H
        EPS = 1e-06

        def _delta_rule(q, k, v, beta):
            b, n, h, hd = q.shape

            def step(S, inp):
                qt, kt, vt, bt = inp
                pred = jnp.einsum('bhk,bhkv->bhv', kt, S)
                delta = bt[..., None] * (vt - pred)
                S = S + jnp.einsum('bhk,bhv->bhkv', kt, delta)
                o = jnp.einsum('bhk,bhkv->bhv', qt, S)
                return (S, o)
            S0 = jnp.zeros((b, h, hd, hd), q.dtype)
            seq = tuple((jnp.moveaxis(t, 1, 0) for t in (q, k, v, beta)))
            _, o = jax.lax.scan(step, S0, seq)
            return jnp.moveaxis(o, 1, 0)
        key = jax.random.key(seed)
        ks = jax.random.split(key, 9)
        s = D ** (-0.5)
        x = jax.random.normal(ks[0], (B, N, D), jnp.float32)
        Wq = jax.random.normal(ks[1], (D, D), jnp.float32) * s
        Wk = jax.random.normal(ks[2], (D, D), jnp.float32) * s
        Wv = jax.random.normal(ks[3], (D, D), jnp.float32) * s
        Wbeta = jax.random.normal(ks[4], (H, D), jnp.float32) * s
        Wg1 = jax.random.normal(ks[5], (HD, D), jnp.float32) * s
        Wg2 = jax.random.normal(ks[6], (D, HD), jnp.float32) * HD ** (-0.5)
        g_norm = jnp.ones((D,), jnp.float32)
        Wo = jax.random.normal(ks[7], (D, D), jnp.float32) * s
        return {'x': x, 'Wq': Wq, 'Wk': Wk, 'Wv': Wv, 'Wbeta': Wbeta, 'Wg1': Wg1, 'Wg2': Wg2, 'g_norm': g_norm, 'Wo': Wo}
    _L0_attn_a_in = _L0_attn_a_setup()

    def _L0_attn_b_setup():
        import jax, jax.numpy as jnp
        import numpy as np
        D_MODEL = 512
        N_QUERY = 4
        N_HEAD = 8
        D_HEAD = D_MODEL // (N_QUERY * N_HEAD)
        D_KV = D_HEAD * N_HEAD
        BATCH, SEQ = (2, 512)
        key = jax.random.key(seed)
        ks = jax.random.split(key, 5)
        w_scale = 1.0 / np.sqrt(D_MODEL).astype(np.float32)
        x = jax.random.normal(ks[0], (BATCH, SEQ, D_MODEL), jnp.float32)
        Wq = jax.random.normal(ks[1], (D_MODEL, D_MODEL), jnp.float32) * w_scale
        Wk = jax.random.normal(ks[2], (D_KV, D_MODEL), jnp.float32) * w_scale
        Wv = jax.random.normal(ks[3], (D_KV, D_MODEL), jnp.float32) * w_scale
        memory = jax.random.normal(ks[4], (D_KV, D_KV), jnp.float32) * 0.02
        memory_norm = jnp.ones((D_KV, 1), jnp.float32)
        memory_weight = jnp.ones((1,), jnp.float32)
        return dict(x=x, Wq=Wq, Wk=Wk, Wv=Wv, memory=memory, memory_norm=memory_norm, memory_weight=memory_weight)
    _L0_attn_b_in = _L0_attn_b_setup()

    def _L0_ffn_setup():
        import jax, jax.numpy as jnp
        import numpy as np
        K = 2
        SCALING = 16.0 / 16.0
        key = jax.random.key(seed)
        ks = jax.random.split(key, 7)
        B, T, D, O, E, R = (2, 1024, 512, 512, 8, 16)
        return {'x': jax.random.normal(ks[0], (B, T, D), dtype=jnp.float32), 'W': jax.random.normal(ks[1], (O, D), dtype=jnp.float32) * (1.0 / np.sqrt(D)), 'b': jax.random.normal(ks[2], (O,), dtype=jnp.float32) * 0.02, 'lora_A': jax.random.normal(ks[3], (E, R, D), dtype=jnp.float32) * (1.0 / np.sqrt(D)), 'lora_B': jax.random.normal(ks[4], (E, O, R), dtype=jnp.float32) * 0.02, 'gate_w': jax.random.normal(ks[5], (E, D), dtype=jnp.float32) * 0.02, 'gate_b': jax.random.normal(ks[6], (E,), dtype=jnp.float32) * 0.02}
    _L0_ffn_in = _L0_ffn_setup()
    _d = {'L0_attn_a_x': _L0_attn_a_in['x'], 'L0_attn_a_Wq': _L0_attn_a_in['Wq'], 'L0_attn_a_Wk': _L0_attn_a_in['Wk'], 'L0_attn_a_Wv': _L0_attn_a_in['Wv'], 'L0_attn_a_Wbeta': _L0_attn_a_in['Wbeta'], 'L0_attn_a_Wg1': _L0_attn_a_in['Wg1'], 'L0_attn_a_Wg2': _L0_attn_a_in['Wg2'], 'L0_attn_a_g_norm': _L0_attn_a_in['g_norm'], 'L0_attn_a_Wo': _L0_attn_a_in['Wo'], 'L0_attn_b_Wq': _L0_attn_b_in['Wq'], 'L0_attn_b_Wk': _L0_attn_b_in['Wk'], 'L0_attn_b_Wv': _L0_attn_b_in['Wv'], 'L0_attn_b_memory': _L0_attn_b_in['memory'], 'L0_attn_b_memory_norm': _L0_attn_b_in['memory_norm'], 'L0_attn_b_memory_weight': _L0_attn_b_in['memory_weight'], 'L0_ffn_W': _L0_ffn_in['W'], 'L0_ffn_b': _L0_ffn_in['b'], 'L0_ffn_lora_A': _L0_ffn_in['lora_A'], 'L0_ffn_lora_B': _L0_ffn_in['lora_B'], 'L0_ffn_gate_w': _L0_ffn_in['gate_w'], 'L0_ffn_gate_b': _L0_ffn_in['gate_b']}
    _x0 = _d['L0_attn_a_x']
    _d['L0_attn_a_x'] = jax.random.normal(jax.random.fold_in(jax.random.key(seed), 1), (16, 512, 512), dtype=_x0.dtype)
    del _x0
    return _d

def reference(L0_attn_a_x, L0_attn_a_Wq, L0_attn_a_Wk, L0_attn_a_Wv, L0_attn_a_Wbeta, L0_attn_a_Wg1, L0_attn_a_Wg2, L0_attn_a_g_norm, L0_attn_a_Wo, L0_attn_b_Wq, L0_attn_b_Wk, L0_attn_b_Wv, L0_attn_b_memory, L0_attn_b_memory_norm, L0_attn_b_memory_weight, L0_ffn_W, L0_ffn_b, L0_ffn_lora_A, L0_ffn_lora_B, L0_ffn_gate_w, L0_ffn_gate_b):

    def _L0_attn_a_ref(x, Wq, Wk, Wv, Wbeta, Wg1, Wg2, g_norm, Wo):
        import jax, jax.numpy as jnp
        import numpy as np
        B, N, D, H = (2, 512, 512, 16)
        HD = D // H
        EPS = 1e-06

        def _delta_rule(q, k, v, beta):
            b, n, h, hd = q.shape

            def step(S, inp):
                qt, kt, vt, bt = inp
                pred = jnp.einsum('bhk,bhkv->bhv', kt, S)
                delta = bt[..., None] * (vt - pred)
                S = S + jnp.einsum('bhk,bhv->bhkv', kt, delta)
                o = jnp.einsum('bhk,bhkv->bhv', qt, S)
                return (S, o)
            S0 = jnp.zeros((b, h, hd, hd), q.dtype)
            seq = tuple((jnp.moveaxis(t, 1, 0) for t in (q, k, v, beta)))
            _, o = jax.lax.scan(step, S0, seq)
            return jnp.moveaxis(o, 1, 0)
        b, n, d = x.shape
        h, hd = (Wbeta.shape[0], d // Wbeta.shape[0])
        silu = jax.nn.silu
        q = silu(x @ Wq.T).reshape(b, n, h, hd)
        k = silu(x @ Wk.T).reshape(b, n, h, hd)
        v = (x @ Wv.T).reshape(b, n, h, hd)
        beta = 2.0 * jax.nn.sigmoid(x @ Wbeta.T)
        k = k * jax.lax.rsqrt(jnp.sum(k * k, axis=-1, keepdims=True) + EPS)
        o = _delta_rule(q, k, v, beta).reshape(b, n, d)
        gate = jax.nn.sigmoid(x @ Wg1.T @ Wg2.T)
        og = (o * gate).reshape(b, n, h, hd)
        rms = jax.lax.rsqrt(jnp.mean(og * og, axis=-1, keepdims=True) + EPS)
        og = (og * rms).reshape(b, n, d) * g_norm
        return og @ Wo.T

    def _L0_attn_b_ref(x, Wq, Wk, Wv, memory, memory_norm, memory_weight):
        import jax, jax.numpy as jnp
        import numpy as np
        D_MODEL = 512
        N_QUERY = 4
        N_HEAD = 8
        D_HEAD = D_MODEL // (N_QUERY * N_HEAD)
        D_KV = D_HEAD * N_HEAD
        BATCH, SEQ = (2, 512)
        b, s, d = x.shape
        q = x @ Wq.T
        k = x @ Wk.T
        v = x @ Wv.T
        qh = q.reshape(b, s, N_QUERY, N_HEAD, D_HEAD)
        kh = k.reshape(b, s, N_HEAD, D_HEAD)
        vh = v.reshape(b, s, N_HEAD, D_HEAD)
        scale = np.float32(1.0 / np.sqrt(np.float32(D_HEAD)))
        scores = jnp.einsum('bsqhd,bthd->bqhst', qh, kh) * scale
        probs = jax.nn.softmax(scores, axis=-1)
        a_dot = jnp.einsum('bqhst,bthd->bsqhd', probs, vh)
        a_dot = a_dot.reshape(b, s, N_QUERY * N_HEAD, D_HEAD)
        sigma_q = jax.nn.elu(q.reshape(b, s, N_QUERY, D_KV))
        a_mem = sigma_q @ memory / (sigma_q @ memory_norm)
        a_mem = a_mem.reshape(b, s, N_QUERY * N_HEAD, D_HEAD)
        w = jax.nn.sigmoid(memory_weight)
        out = a_dot * (1.0 - w) + a_mem * w
        return out.reshape(b, s, D_MODEL)

    def _L0_ffn_ref(x, W, b, lora_A, lora_B, gate_w, gate_b):
        import jax, jax.numpy as jnp
        import numpy as np
        K = 2
        SCALING = 16.0 / 16.0
        orig_shape = x.shape
        D = orig_shape[-1]
        O = W.shape[0]
        x_flat = x.reshape(-1, D)
        base = x_flat @ W.T + b
        logits = x_flat @ gate_w.T + gate_b
        topk_logits, topk_idx = jax.lax.top_k(logits, K)
        gates = jax.nn.softmax(topk_logits, axis=-1)
        xA = jnp.einsum('nd,erd->ner', x_flat, lora_A)
        delta_all = jnp.einsum('ner,eor->neo', xA, lora_B)
        delta_topk = jnp.take_along_axis(delta_all, topk_idx[:, :, None], axis=1)
        lora_update = jnp.sum(delta_topk * gates[:, :, None], axis=1)
        out = base + SCALING * lora_update
        return out.reshape(*orig_shape[:-1], O)
    x = L0_attn_a_x
    x = x + _L0_attn_a_ref(_layernorm(x, axis=-1), L0_attn_a_Wq, L0_attn_a_Wk, L0_attn_a_Wv, L0_attn_a_Wbeta, L0_attn_a_Wg1, L0_attn_a_Wg2, L0_attn_a_g_norm, L0_attn_a_Wo)
    x = x + _L0_ffn_ref(_layernorm(x, axis=-1), L0_ffn_W, L0_ffn_b, L0_ffn_lora_A, L0_ffn_lora_B, L0_ffn_gate_w, L0_ffn_gate_b)
    x = x + _L0_attn_b_ref(_layernorm(x, axis=-1), L0_attn_b_Wq, L0_attn_b_Wk, L0_attn_b_Wv, L0_attn_b_memory, L0_attn_b_memory_norm, L0_attn_b_memory_weight)
    x = x + _L0_ffn_ref(_layernorm(x, axis=-1), L0_ffn_W, L0_ffn_b, L0_ffn_lora_A, L0_ffn_lora_B, L0_ffn_gate_w, L0_ffn_gate_b)
    return x

_drawn_inputs = setup_inputs


def setup_inputs(seed=0):
    import zlib

    import numpy as np

    out = dict(_drawn_inputs(seed))
    spreads = {'L0_attn_a_g_norm': (1.0, 0.2), 'L0_attn_b_memory_norm': (1.0, 0.2)}
    factors = {'L0_attn_b_Wk': 4.941, 'L0_attn_b_Wv': 4.082}
    for name, (base, spread) in spreads.items():
        noise = np.random.default_rng([zlib.crc32(name.encode()), seed]).standard_normal(out[name].shape)
        drawn = base * np.exp(spread * noise) if base else spread * noise
        out[name] = jnp.asarray(drawn.astype(out[name].dtype))
    for name, factor in factors.items():
        out[name] = (out[name] * factor).astype(out[name].dtype)
    return out
```

```python
from contextlib import ExitStack

import concourse.bass as bass
from concourse import mybir

F32 = mybir.dt.float32
F32R = mybir.dt.float32r
ALU = mybir.AluOpType
ACT = mybir.ActivationFunctionType
AX = mybir.AxisListType

P = 128
KT = 4
D = P * KT
H = 16
HD = D // H
HPT = P // HD
SPAN = 256
TS = SPAN // P
C = 64
NB = 32
ROWS_GB = 112
LN_EPS = 1e-5
EPS = 1e-6


def split3(pe, out, a_hi, a_lo, b_hi, b_lo, first, last):
    pe.matmul(out, a_hi, b_hi, start=first, stop=False)
    pe.matmul(out, a_hi, b_lo, start=False, stop=False)
    return pe.matmul(out, a_lo, b_hi, start=False, stop=last)


def delta_rule_layer(nc, dims, x_in, w_main, w_gb, w_g2, g_norm, ident_in, masks_in, ones_in, out):
    NBATCH, SEQ = dims
    SPB = SEQ // SPAN

    tri_dram = nc.dram_tensor("tri_dram", [TS * 4, H, NB, NB], F32, kind="Internal").ap()
    beta_dram = nc.dram_tensor("beta_dram", [TS * 4, H, NB], F32, kind="Internal").ap()
    inv_dram = nc.dram_tensor("inv_dram", [TS * 4, H, NB, NB], F32, kind="Internal").ap()

    with ExitStack() as ctx:
        def sb(name, shape, dt=F32):
            return ctx.enter_context(nc.sbuf_tensor(name, shape, dt))

        def sem(name):
            return ctx.enter_context(nc.semaphore(name))

        bank = [ctx.enter_context(nc.psum_tensor(f"span_bank{n}", [P, 512], F32)) for n in range(8)]

        NW = 4
        w_hi = sb("w_hi", [P, NW, KT, D], F32R)
        w_lo = sb("w_lo", [P, NW, KT, D], F32R)
        gb_hi = sb("gb_hi", [P, KT, ROWS_GB], F32R)
        gb_lo = sb("gb_lo", [P, KT, ROWS_GB], F32R)
        g2_stack = sb("g2_stack", [3 * HD, D], F32R)
        gnorm_half = sb("gnorm_half", [P, KT])
        ident = sb("ident", [P, P])
        masks = sb("masks", [P, 2 * C])
        head_ones = sb("head_ones", [P, P])
        eps_t = sb("eps_t", [P, 1])
        minus_half = sb("minus_half", [P, TS])
        ln_eps = sb("ln_eps", [P, TS])

        x_sp = sb("x_sp", [P, 2, TS, D])
        stats = sb("stats", [P, TS, 6])
        mv = sb("mv", [P, TS, 2])
        var_eps = sb("var_eps", [P, TS])
        rstd = sb("rstd", [P, TS])
        xn = sb("xn", [P, TS, D])
        x_hi = sb("x_hi", [P, KT, SPAN], F32R)
        x_lo = sb("x_lo", [P, KT, SPAN], F32R)
        k_silu = sb("k_silu", [P, KT, SPAN])
        sq = sb("sq", [P, KT, SPAN])
        r_norm = sb("r_norm", [P, KT, SPAN])
        kq = sb("kq", [P, KT, 2, SPAN])
        g1_stack = sb("g1_stack", [3 * HD, SPAN], F32R)
        beta_t = sb("beta_t", [P, SPAN])
        gate = sb("gate", [P, KT, SPAN])
        rhs = sb("rhs", [P, TS, H, 2 * HD])
        tri = sb("tri", [P, TS, KT, HPT, 2 * C])
        stage = tri[:, :, :, :, :].rearrange("p t g e i -> p (t g e i)")[:, 0:KT * D]
        lane_l = sb("lane_l", [P, NB, NB])
        lane_b = sb("lane_b", [P, NB])
        lane_a = sb("lane_a", [P, NB, NB])
        lane_t = sb("lane_t", [P, NB, NB])
        lane_tb = sb("lane_tb", [P, NB, NB])
        lane_p = sb("lane_p", [P, NB * NB])
        inv_b = sb("inv_b", [P, TS, H, NB])
        uw = sb("uw", [P, TS, H, 2 * HD])
        rhs2 = sb("rhs2", [P, TS, H, 2 * HD])
        q_eff = sb("q_eff", [P, KT, SPAN])
        gh = sb("gh", [P, 2, TS, KT, 2 * HD])
        state = sb("state", [P, SPB * 4 + 1, KT * HD])
        s_plus = sb("s_plus", [P, KT * HD])
        og = sb("og", [P, KT, SPAN])
        o_hi = sb("o_hi", [P, KT, SPAN], F32R)
        o_lo = sb("o_lo", [P, KT, SPAN], F32R)

        w_in = sem("w_in"); w_split = sem("w_split"); c_in = sem("c_in"); pool_consts = sem("pool_consts"); dve_consts = sem("dve_consts")
        x_loaded = sem("x_loaded"); var_ready = sem("var_ready"); rstd_ready = sem("rstd_ready")
        xn_ready = sem("xn_ready"); xT_ready = sem("xT_ready"); xhi_ready = sem("xhi_ready")
        xlo_ready = sem("xlo_ready"); kproj = sem("kproj"); ksilu_ready = sem("ksilu_ready")
        gb_proj = sem("gb_proj"); g1hi_ready = sem("g1hi_ready"); g1_ready = sem("g1_ready")
        betat_ready = sem("betat_ready"); beta_ready = sem("beta_ready")
        qproj = sem("qproj"); q_ready = sem("q_ready"); vproj = sem("vproj"); v_ready = sem("v_ready")
        sq_ready = sem("sq_ready"); ss_ready = sem("ss_ready"); rk_ready = sem("rk_ready"); k_ready = sem("k_ready")
        gate_proj = sem("gate_proj"); gate_ready = sem("gate_ready")
        ktok = sem("ktok"); rhs_k_ready = sem("rhs_k_ready")
        kk_ready = sem("kk_ready"); tri_ready = sem("tri_ready")
        tri_out = sem("tri_out"); lane_in = sem("lane_in"); inv_ready = sem("inv_ready")
        inv_out = sem("inv_out"); inv_in = sem("inv_in")
        u0_mm = sem("u0_mm"); u0_ready = sem("u0_ready"); p_mm = sem("p_mm"); rhs2_ready = sem("rhs2_ready")
        u1_mm = sem("u1_mm"); uw_ready = sem("uw_ready")
        mw_mm = sem("mw_mm"); qeff_ready = sem("qeff_ready"); gh_mm = sem("gh_mm"); gh_ready = sem("gh_ready")
        chain_mm = sem("chain_mm"); state_ready = sem("state_ready")
        o_mm = sem("o_mm"); og_ready = sem("og_ready"); sq2_ready = sem("sq2_ready"); ms_ready = sem("ms_ready")
        ro_ready = sem("ro_ready"); ogn_ready = sem("ogn_ready"); ohi_ready = sem("ohi_ready"); olo_ready = sem("olo_ready")
        wo_mm = sem("wo_mm"); x2_ready = sem("x2_ready"); x2_stored = sem("x2_stored")
        dve_own = sem("dve_own"); act_own = sem("act_own"); pool_own = sem("pool_own")

        x_rows = x_in.rearrange("b (s t p) d -> b s p t d", p=P, t=TS)
        out_rows = out.rearrange("b (s t p) d -> b s p t d", p=P, t=TS)

        def at(b, s, per, k):
            return b * (SPB * per) + (s * per + k)

        CREDIT, STORE_CREDIT = 1, 32

        block = ctx.enter_context(nc.Block())

        @block.sync
        def _(sp):
            sp.sem_inc(x2_ready, CREDIT)
            sp.sem_inc(x2_stored, STORE_CREDIT)
            for n in range(NW):
                if n:
                    sp.wait_ge(w_split, 2 * n)
                sp.dma_start(stage[:, :], w_main[n]).then_inc(w_in, 16)
            sp.wait_ge(w_split, 2 * NW)
            sp.dma_start(stage[:, 0:KT * ROWS_GB], w_gb).then_inc(w_in, 16)
            sp.dma_start(stage[0:3 * HD, D:2 * D], w_g2).then_inc(w_in, 16)
            sp.dma_start(ident[:, :], ident_in).then_inc(c_in, 16)
            sp.dma_start(masks[:, :], masks_in).then_inc(c_in, 16)
            sp.dma_start(head_ones[:, :], ones_in).then_inc(c_in, 16)
            sp.dma_start(gnorm_half[:, :], g_norm).then_inc(c_in, 16)

            def load_x(b, s, slot):
                sp.dma_start(x_sp[:, slot, :, :], x_rows[b, s]).then_inc(x_loaded, 16)

            with sp.Fori(0, NBATCH) as b:
                for s in range(SPB):
                    sp.wait_ge(x2_stored, at(b, s, 16, STORE_CREDIT - 16))
                    load_x(b, s, s)
                    for t in range(TS):
                        sp.wait_ge(tri_ready, at(b, s, TS * HPT, (t + 1) * HPT))
                        for pb in range(4):
                            i0 = NB * (pb % 2)
                            sp.dma_start(tri_dram[t * 4 + pb].rearrange("h j i -> j h i"),
                                         tri[NB * pb:NB * pb + NB, t, :, :, i0:i0 + NB].rearrange("j g e i -> j (g e) i")
                                         ).then_inc(tri_out, 16)
                    sp.wait_ge(beta_ready, at(b, s, 1, 1))
                    sp.dma_start(beta_dram.rearrange("u h i -> h u i"),
                                 beta_t[96:96 + H, :].rearrange("h (u i) -> h u i", i=NB)).then_inc(tri_out, 16)
                    sp.wait_ge(tri_out, at(b, s, 16 * (TS * 4 + 1), 16 * (TS * 4 + 1)))
                    sp.dma_start(lane_l[:, :, :], tri_dram.rearrange("u h j i -> (u h) j i")).then_inc(lane_in, 16)
                    sp.dma_start(lane_b[:, :], beta_dram.rearrange("u h i -> (u h) i")).then_inc(lane_in, 16)
                    sp.wait_ge(inv_ready, at(b, s, 1, 1))
                    sp.dma_start(inv_dram.rearrange("u h j i -> (u h) j i"), lane_tb[:, :, :]).then_inc(inv_out, 16)
                    sp.wait_ge(inv_out, at(b, s, 16, 16))
                    for t in range(TS):
                        for pb in range(4):
                            sp.dma_start(inv_b[NB * pb:NB * pb + NB, t, :, :],
                                         inv_dram[t * 4 + pb].rearrange("h j i -> j h i")).then_inc(inv_in, 16)
                    sp.wait_ge(x2_ready, at(b, s, TS, CREDIT + TS))
                    sp.dma_start(out_rows[b, s], x_sp[:, s, :, :]).then_inc(x2_stored, 16)
            sp.wait_ge(x2_stored, STORE_CREDIT + NBATCH * SPB * 16)

        @block.gpsimd
        def _(pool):
            pool.memset(minus_half[:, :], -0.5).then_inc(pool_consts, 1)
            pool.memset(ln_eps[:, :], LN_EPS).then_inc(pool_consts, 1)
            pool.memset(state[:, 0, :], 0.0).then_inc(pool_consts, 1)
            pool.memset(eps_t[:, :], EPS).then_inc(pool_consts, 1)
            pool.wait_ge(pool_consts, 4)
            with pool.Fori(0, NBATCH) as b:
                for s in range(SPB):
                    pool.wait_ge(var_ready, at(b, s, TS, TS))
                    pool.tensor_tensor(var_eps[:, :], mv[:, :, 1], ln_eps[:, :], ALU.add).then_inc(pool_own, 1)
                    pool.wait_ge(pool_own, at(b, s, 1, 1))
                    pool.tensor_tensor(rstd[:, :], var_eps[:, :], minus_half[:, :], ALU.pow).then_inc(rstd_ready, 1)
                    for n in range(2):
                        pool.wait_ge(ksilu_ready, at(b, s, 2, n + 1))
                        v = k_silu[:, 2 * n:2 * n + 2, :]
                        pool.tensor_tensor(sq[:, 2 * n:2 * n + 2, :], v, v, ALU.mult).then_inc(sq_ready, 1)
                    for t in range(TS):
                        pool.wait_ge(og_ready, at(b, s, 4, 2 * t + 2))
                        v = og[:, :, P * t:P * t + P]
                        pool.tensor_tensor(sq[:, :, P * t:P * t + P], v, v, ALU.mult).then_inc(sq2_ready, 1)
                    pool.wait_ge(ohi_ready, at(b, s, 1, 1))
                    pool.tensor_tensor(o_lo[:, :, :], og[:, :, :], o_hi[:, :, :].bitcast(F32), ALU.subtract).then_inc(olo_ready, 1)

        @block.scalar
        def _(act):
            for n in range(NW):
                act.wait_ge(w_in, 16 * (n + 1))
                act.activation(w_hi[:, n, :, :].rearrange("p k n -> p (k n)"), stage[:, :], ACT.Copy).then_inc(w_split, 1)
            act.wait_ge(w_in, 16 * (NW + 2))
            act.activation(gb_hi[:, :, :].rearrange("p k n -> p (k n)"), stage[:, 0:KT * ROWS_GB], ACT.Copy).then_inc(w_split, 1)
            act.activation(g2_stack[:, :], stage[0:3 * HD, D:2 * D], ACT.Copy).then_inc(w_split, 1)
            act.wait_ge(pool_consts, 4)
            with act.Fori(0, NBATCH) as b:
                for s in range(SPB):
                    for n in range(2):
                        act.wait_ge(xT_ready, at(b, s, 2, n + 1))
                        act.activation(x_hi[:, 2 * n:2 * n + 2, :], bank[n][:, :], ACT.Copy).then_inc(xhi_ready, 1)
                    for n in range(2):
                        act.wait_ge(kproj, at(b, s, 2, n + 1))
                        act.activation(k_silu[:, 2 * n:2 * n + 2, :], bank[2 + n][:, :], ACT.Silu).then_inc(ksilu_ready, 1)
                    act.wait_ge(gb_proj, at(b, s, 1, 1))
                    act.activation(g1_stack[:, :], bank[0][0:3 * HD, 0:SPAN], ACT.Copy).then_inc(g1hi_ready, 1)
                    act.activation(beta_t[96:96 + H, :], bank[0][96:96 + H, 0:SPAN], ACT.Tanh, scale=0.5).then_inc(betat_ready, 1)
                    for n in range(2):
                        act.wait_ge(qproj, at(b, s, 2, n + 1))
                        act.activation(kq[:, 2 * n:2 * n + 2, 1, :], bank[1 + n][:, :].rearrange("p (g i) -> p g i", g=2),
                                       ACT.Silu).then_inc(q_ready, 1)
                    for n in range(2):
                        act.wait_ge(gate_proj, at(b, s, 2, n + 1))
                        act.activation(gate[:, 2 * n:2 * n + 2, :], bank[3 - 3 * n][:, :], ACT.Tanh, scale=0.5).then_inc(gate_ready, 1)
                    for n in range(2):
                        v = r_norm[:, 2 * n:2 * n + 2, :]
                        act.wait_ge(ss_ready, at(b, s, 2, n + 1))
                        act.activation(v, bank[1 + n][:, :], ACT.Ln, bias=eps_t[:, 0:1]).then_inc(act_own, 1)
                    for n in range(2):
                        v = r_norm[:, 2 * n:2 * n + 2, :]
                        act.wait_ge(act_own, at(b, s, 4, n + 1))
                        act.activation(v, v, ACT.Exp, scale=-0.5).then_inc(rk_ready, 1)
                    for t in range(TS):
                        act.wait_ge(ktok, at(b, s, TS, t + 1))
                        act.activation(rhs[:, t, :, HD:2 * HD], bank[1 + t][:, :].rearrange("p (h e) -> p h e", h=H),
                                       ACT.Copy).then_inc(rhs_k_ready, 1)
                    for t in range(TS):
                        act.wait_ge(u0_mm, at(b, s, TS, t + 1))
                        for n in range(2):
                            act.activation(uw[:, t, 8 * n:8 * n + 8, :], bank[4 + 2 * t + n][:, :].rearrange("p (h e) -> p h e", h=8),
                                           ACT.Copy).then_inc(u0_ready, 1)
                    for t in range(TS):
                        act.wait_ge(u1_mm, at(b, s, TS, t + 1))
                        for n in range(2):
                            act.activation(uw[:, t, 8 * n:8 * n + 8, :], bank[4 + 2 * t + n][:, :].rearrange("p (h e) -> p h e", h=8),
                                           ACT.Copy).then_inc(uw_ready, 1)
                    for half in range(2):
                        act.wait_ge(gh_mm, at(b, s, 2, half + 1))
                        act.activation(gh[:, half, :, :, :], bank[6 + half][:, :].rearrange("p (t g e) -> p t g e", t=TS, g=KT),
                                       ACT.Copy).then_inc(gh_ready, 1)
                    for n in range(2):
                        v = r_norm[:, 2 * n:2 * n + 2, :]
                        act.wait_ge(ms_ready, at(b, s, 2, n + 1))
                        act.activation(v, bank[3 - 3 * n][:, :], ACT.Ln, bias=eps_t[:, 0:1], scale=1.0 / (4 * HD)).then_inc(act_own, 1)
                    for n in range(2):
                        v = r_norm[:, 2 * n:2 * n + 2, :]
                        act.wait_ge(act_own, at(b, s, 4, 3 + n))
                        act.activation(v, v, ACT.Exp, scale=-0.5).then_inc(ro_ready, 1)
                    act.wait_ge(ogn_ready, at(b, s, KT, KT))
                    act.activation(o_hi[:, :, :], og[:, :, :], ACT.Copy).then_inc(ohi_ready, 1)

        @block.tensor
        def _(pe):
            pe.wait_ge(w_split, 2 * (NW + 2))
            pe.wait_ge(c_in, 64)
            pe.wait_ge(pool_consts, 4)
            pe.wait_ge(dve_consts, 2)
            awaited = pe.alloc_register("awaited")
            with pe.Fori(0, NBATCH) as b:
                for s in range(SPB):
                    def after(value):
                        pe.reg_mov(awaited, value)
                        pe.wait_ge(pool_consts, 4)
                        return awaited

                    def project(out_ap, w, g):
                        for k in range(KT):
                            last = split3(pe, out_ap, w_hi[:, w, k, P * g:P * g + P], w_lo[:, w, k, P * g:P * g + P],
                                          x_hi[:, k, :], x_lo[:, k, :], k == 0, k == KT - 1)
                        return last

                    pe.wait_ge(xn_ready, at(b, s, TS, TS))
                    pe.wait_ge(x2_ready, at(b, s, TS, CREDIT))
                    for n in range(2):
                        for g in range(2):
                            for t in range(TS):
                                k = 2 * n + g
                                last = pe.transpose(bank[n][:, SPAN * g + P * t:SPAN * g + P * t + P],
                                                    xn[:, t, P * k:P * k + P], ident[:, :])
                        last.then_inc(xT_ready, 1)
                    pe.wait_ge(xhi_ready, at(b, s, 2, 2))
                    pe.wait_ge(xlo_ready, at(b, s, 2, 2))
                    for n in range(2):
                        for g in range(2):
                            last = project(bank[2 + n][:, SPAN * g:SPAN * g + SPAN], 0, 2 * n + g)
                        last.then_inc(kproj, 1)
                    for k in range(KT):
                        last = split3(pe, bank[0][0:ROWS_GB, 0:SPAN], gb_hi[:, k, :], gb_lo[:, k, :],
                                      x_hi[:, k, :], x_lo[:, k, :], k == 0, k == KT - 1)
                    last.then_inc(gb_proj, 1)
                    for n in range(2):
                        if n:
                            pe.wait_ge(ksilu_ready, at(b, s, 2, 1))
                        for g in range(2):
                            last = project(bank[1 + n][:, SPAN * g:SPAN * g + SPAN], 1, 2 * n + g)
                        last.then_inc(qproj, 1)
                    for t in range(TS):
                        if t == 0:
                            pe.wait_ge(ksilu_ready, at(b, s, 2, 2))
                        else:
                            pe.wait_ge(betat_ready, at(b, s, 1, 1))
                            pe.wait_ge(g1_ready, at(b, s, 1, 1))
                        for k in range(KT):
                            last = split3(pe, bank[3 - 3 * t][:, :], x_hi[:, k, P * t:P * t + P], x_lo[:, k, P * t:P * t + P],
                                          w_hi[:, 2, k, :], w_lo[:, 2, k, :], k == 0, k == KT - 1)
                        last.then_inc(vproj, 1)
                    for n in range(2):
                        pe.wait_ge(sq_ready, at(b, s, 2, n + 1))
                        pe.wait_ge(q_ready, at(b, s, 2, n + 1))
                        pe.matmul(bank[1 + n][:, :], head_ones[:, :], sq[:, 2 * n:2 * n + 2, :],
                                  start=True, stop=True).then_inc(ss_ready, 1)
                    for n in range(2):
                        pe.wait_ge(v_ready, at(b, s, TS, n + 1))
                        for g in range(2):
                            f = 2 * n + g
                            last = pe.matmul(bank[3 - 3 * n][:, SPAN * g:SPAN * g + SPAN], g2_stack[:, P * f:P * f + P],
                                             g1_stack[:, :], start=True, stop=True)
                        last.then_inc(gate_proj, 1)
                    for t in range(TS):
                        pe.wait_ge(k_ready, at(b, s, 2, 2))
                        pe.wait_ge(rk_ready, at(b, s, 2, 2))
                        for g in range(KT):
                            last = pe.transpose(bank[1 + t][:, P * g:P * g + P], kq[:, g, 0, P * t:P * t + P], ident[:, :])
                        last.then_inc(ktok, 1)

                    for t in range(TS):
                        for e in range(HPT):
                            if t:
                                pe.wait_ge(tri_ready, after(at(b, s, TS * HPT, e + 1)))
                            rows = slice(HD * e, HD * e + HD)
                            for g in range(KT):
                                for half in range(2):
                                    i0 = P * t + C * half
                                    last = pe.matmul(bank[4 + e][C * half:C * half + C, 2 * C * g:2 * C * g + 2 * C],
                                                     kq[rows, g, 0, i0:i0 + C], kq[rows, g, :, i0:i0 + C],
                                                     start=True, stop=True)
                            last.then_inc(kk_ready, 1)

                    pe.wait_ge(inv_in, at(b, s, 16 * TS * 4, 16 * TS * 4))
                    pe.wait_ge(rhs_k_ready, at(b, s, TS, TS))
                    pe.wait_ge(v_ready, at(b, s, TS, TS))
                    pe.wait_ge(tri_ready, after(at(b, s, TS * HPT, TS * HPT)))

                    def blocks(t, lower, weights, moving):
                        for h in range(H):
                            for half in range(2):
                                src = NB * (2 * half + (1 if lower == 2 else 0))
                                dst = NB * (2 * half + (1 if lower else 0))
                                last = pe.matmul(bank[4 + 2 * t + h // 8][dst:dst + NB, 2 * HD * (h % 8):2 * HD * (h % 8) + 2 * HD],
                                                 weights(h, src), moving[src:src + NB, t, h, :], start=True, stop=True)
                        return last

                    for t in range(TS):
                        blocks(t, 0, lambda h, r: inv_b[r:r + NB, t, h, :], rhs).then_inc(u0_mm, 1)
                    for t in range(TS):
                        pe.wait_ge(u0_ready, after(at(b, s, 2 * TS, 2 * t + 2)))
                        blocks(t, 1, lambda h, r: tri[r:r + NB, t, h // HPT, h % HPT, NB:2 * NB], uw).then_inc(p_mm, 1)
                    for t in range(TS):
                        pe.wait_ge(rhs2_ready, after(at(b, s, 2 * TS, 2 * t + 2)))
                        blocks(t, 2, lambda h, r: inv_b[r:r + NB, t, h, :], rhs2).then_inc(u1_mm, 1)

                    pe.wait_ge(uw_ready, after(at(b, s, 2 * TS, 2 * TS)))
                    for half in range(2):
                        rows = slice(C * half, C * half + C)
                        for t in range(TS):
                            for h in range(H):
                                g, e = h // HPT, h % HPT
                                last = pe.matmul(bank[4 + half][HD * e:HD * e + HD, (t * KT + g) * C:(t * KT + g) * C + C],
                                                 uw[rows, t, h, HD:2 * HD], tri[rows, t, g, e, C:2 * C], start=True, stop=True)
                        last.then_inc(mw_mm, 1)
                    for half in range(2):
                        rows = slice(C * half, C * half + C)
                        for t in range(TS):
                            for h in range(H):
                                g, e = h // HPT, h % HPT
                                c0 = (t * KT + g) * 2 * HD
                                o = bank[6 + half][HD * e:HD * e + HD, :]
                                pe.matmul(o[:, c0:c0 + HD], uw[rows, t, h, HD:2 * HD], rhs[rows, t, h, HD:2 * HD],
                                          start=True, stop=True)
                                last = pe.matmul(o[:, c0 + HD:c0 + 2 * HD], rhs[rows, t, h, HD:2 * HD], uw[rows, t, h, 0:HD],
                                                 start=True, stop=True)
                        last.then_inc(gh_mm, 1)

                    for c in range(2 * TS):
                        t, half = c // 2, c % 2
                        if c == 0:
                            done = after(at(b, s, 2, 2))
                            pe.wait_ge(gh_ready, done)
                            pe.wait_ge(qeff_ready, done)
                        else:
                            pe.wait_ge(state_ready, after(at(b, s, 4, c)))
                        for h in range(H):
                            g, e = h // HPT, h % HPT
                            r = slice(HD * e, HD * e + HD)
                            last = pe.matmul(bank[4][r, P * c + HD * g:P * c + HD * g + HD], gh[r, half, t, g, 0:HD],
                                             state[r, 4 * s + c, HD * g:HD * g + HD], start=True, stop=True)
                        last.then_inc(chain_mm, 1)
                        rows = slice(C * half, C * half + C)
                        o = [bank[6 + half][HD * (h % HPT):HD * (h % HPT) + HD,
                                            C * (KT * t + h // HPT):C * (KT * t + h // HPT) + C] for h in range(H)]
                        for h in range(H):
                            g, e = h // HPT, h % HPT
                            pe.matmul(o[h], uw[rows, t, h, 0:HD], tri[rows, t, g, e, C:2 * C],
                                      start=g == 0, stop=False, skip_group_check=True)
                        for h in range(H):
                            g, e = h // HPT, h % HPT
                            r = slice(HD * e, HD * e + HD)
                            last = pe.matmul(o[h], state[r, 4 * s + c, HD * g:HD * g + HD],
                                             q_eff[r, g, P * t + C * half:P * t + C * half + C],
                                             start=False, stop=g == KT - 1, skip_group_check=True)
                        last.then_inc(o_mm, 1)

                    pe.wait_ge(sq2_ready, at(b, s, TS, TS))
                    pe.wait_ge(gate_ready, at(b, s, 2, 2))
                    for n in range(2):
                        pe.matmul(bank[3 - 3 * n][:, :], head_ones[:, :], sq[:, 2 * n:2 * n + 2, :],
                                  start=True, stop=True).then_inc(ms_ready, 1)
                    pe.wait_ge(ohi_ready, at(b, s, 1, 1))
                    pe.wait_ge(olo_ready, at(b, s, 1, 1))
                    for t in range(TS):
                        for k in range(KT):
                            last = split3(pe, bank[1 + t][:, :], o_hi[:, k, P * t:P * t + P], o_lo[:, k, P * t:P * t + P],
                                          w_hi[:, 3, k, :], w_lo[:, 3, k, :], k == 0, k == KT - 1)
                        last.then_inc(wo_mm, 1)

        @block.vector
        def _(dve):
            for n in range(NW):
                dve.wait_ge(w_split, 2 * n + 1)
                dve.tensor_tensor(w_lo[:, n, :, :].rearrange("p k n -> p (k n)"), stage[:, :],
                                  w_hi[:, n, :, :].rearrange("p k n -> p (k n)").bitcast(F32), ALU.subtract).then_inc(w_split, 1)
            dve.wait_ge(w_split, 2 * NW + 2)
            dve.tensor_tensor(gb_lo[:, :, :].rearrange("p k n -> p (k n)"), stage[:, 0:KT * ROWS_GB],
                              gb_hi[:, :, :].rearrange("p k n -> p (k n)").bitcast(F32), ALU.subtract).then_inc(w_split, 1)
            lo = slice(2 * HD, 3 * HD)
            dve.tensor_tensor(g2_stack[lo, :], stage[lo, D:2 * D], g2_stack[lo, :].bitcast(F32), ALU.subtract).then_inc(w_split, 1)
            dve.wait_ge(c_in, 64)
            dve.tensor_scalar(gnorm_half[:, :], gnorm_half[:, :], 0.5, None, ALU.mult).then_inc(dve_consts, 1)
            dve.memset(lane_t[:, :, :], 0.0).then_inc(dve_own, 1)
            dve.wait_ge(dve_own, 1)
            dve.memset(lane_t[:, :, :].rearrange("p j i -> p (j i)")[:, 0:NB * NB:NB + 1], 1.0).then_inc(dve_consts, 1)
            dve.wait_ge(dve_consts, 2)
            dve.wait_ge(pool_consts, 4)
            dve.sem_clear(dve_own)
            with dve.Fori(0, NBATCH) as b:
                for s in range(SPB):
                    own = 0
                    dve.wait_ge(x_loaded, at(b, s, 16, 16))
                    for t in range(TS):
                        dve.bn_stats(stats[:, t, :], x_sp[:, s, t, :]).then_inc(dve_own, 1)
                        own += 1
                    for t in range(TS):
                        dve.wait_ge(dve_own, t + 1)
                        dve.bn_aggr(mv[:, t, :], stats[:, t, :]).then_inc(var_ready, 1)
                    dve.wait_ge(var_ready, at(b, s, TS, TS))
                    dve.wait_ge(rstd_ready, at(b, s, 1, 1))
                    for t in range(TS):
                        dve.tensor_scalar(xn[:, t, :], x_sp[:, s, t, :], mv[:, t, 0:1], rstd[:, t:t + 1],
                                          ALU.subtract, ALU.mult).then_inc(xn_ready, 1)
                    for n in range(2):
                        dve.wait_ge(xhi_ready, at(b, s, 2, n + 1))
                        dve.tensor_tensor(x_lo[:, 2 * n:2 * n + 2, :], bank[n][:, :].rearrange("p (g i) -> p g i", g=2),
                                          x_hi[:, 2 * n:2 * n + 2, :].bitcast(F32), ALU.subtract).then_inc(xlo_ready, 1)
                    dve.wait_ge(g1hi_ready, at(b, s, 1, 1))
                    r = slice(HD, 2 * HD)
                    dve.tensor_tensor(g1_stack[r, :], bank[0][r, 0:SPAN], g1_stack[r, :].bitcast(F32), ALU.subtract).then_inc(g1_ready, 1)
                    dve.wait_ge(betat_ready, at(b, s, 1, 1))
                    dve.tensor_scalar(beta_t[96:96 + H, :], beta_t[96:96 + H, :], 1.0, None, ALU.add).then_inc(beta_ready, 1)
                    for t in range(TS):
                        dve.wait_ge(vproj, at(b, s, TS, t + 1))
                        dve.tensor_copy(rhs[:, t, :, 0:HD], bank[3 - 3 * t][:, :].rearrange("p (h e) -> p h e", h=H)).then_inc(v_ready, 1)
                    for n in range(2):
                        dve.wait_ge(rk_ready, at(b, s, 2, n + 1))
                        g = slice(2 * n, 2 * n + 2)
                        dve.tensor_tensor(kq[:, g, 0, :], k_silu[:, g, :], r_norm[:, g, :], ALU.mult).then_inc(k_ready, 1)
                    m = masks[:, :].rearrange("p (o i) -> p o i", o=1).to_broadcast([P, KT, 2 * C])
                    for t in range(TS):
                        for e in range(HPT):
                            dve.wait_ge(kk_ready, at(b, s, TS * HPT, t * HPT + e + 1))
                            dve.tensor_tensor(tri[:, t, :, e, :], bank[4 + e][:, :].rearrange("p (g i) -> p g i", g=KT), m,
                                              ALU.mult).then_inc(tri_ready, 1)
                    dve.wait_ge(lane_in, at(b, s, 32, 32))
                    dve.scalar_tensor_tensor(lane_a[:, :, :], lane_l[:, :, :], -1.0,
                                             lane_b[:, :].rearrange("p (o i) -> p o i", o=1).to_broadcast([P, NB, NB]),
                                             ALU.mult, ALU.mult).then_inc(dve_own, 1)
                    own += 1
                    for i in range(1, NB):
                        col = lane_a[:, 0:i, i:i + 1].rearrange("p m o -> p o m").to_broadcast([P, i, i])
                        prod = lane_p[:, 0:i * i].rearrange("p (j m) -> p j m", j=i)
                        dve.wait_ge(dve_own, own)
                        dve.tensor_tensor(prod, col, lane_t[:, 0:i, 0:i], ALU.mult).then_inc(dve_own, 1)
                        own += 1
                        dve.wait_ge(dve_own, own)
                        dve.tensor_reduce(lane_t[:, 0:i, i], prod, AX.X, ALU.add).then_inc(dve_own, 1)
                        own += 1
                    dve.wait_ge(dve_own, own)
                    dve.tensor_tensor(lane_tb[:, :, :], lane_t[:, :, :],
                                      lane_b[:, :].rearrange("p (j o) -> p j o", o=1).to_broadcast([P, NB, NB]),
                                      ALU.mult).then_inc(inv_ready, 1)
                    for t in range(TS):
                        dve.wait_ge(p_mm, at(b, s, TS, t + 1))
                        for n in range(2):
                            hs = slice(8 * n, 8 * n + 8)
                            dve.tensor_tensor(rhs2[:, t, hs, :], rhs[:, t, hs, :],
                                              bank[4 + 2 * t + n][:, :].rearrange("p (h e) -> p h e", h=8),
                                              ALU.subtract).then_inc(rhs2_ready, 1)
                    for half in range(2):
                        dve.wait_ge(mw_mm, at(b, s, 2, half + 1))
                        qv = kq[:, :, 1, :].rearrange("p g (t f i) -> p t g f i", t=TS, f=2)[:, :, :, half, :]
                        ov = q_eff[:, :, :].rearrange("p g (t f i) -> p t g f i", t=TS, f=2)[:, :, :, half, :]
                        pv = bank[4 + half][:, :].rearrange("p (t g i) -> p t g i", t=TS, g=KT)
                        for t in range(TS):
                            last = dve.tensor_tensor(ov[:, t], qv[:, t], pv[:, t], ALU.subtract)
                        last.then_inc(qeff_ready, 1)
                    for c in range(2 * TS):
                        t, half = c // 2, c % 2
                        if c == 0:
                            dve.wait_ge(gh_ready, at(b, s, 2, 2))
                        if s or c:
                            dve.wait_ge(state_ready, at(b, s, 4, c))
                        dve.tensor_tensor(s_plus[:, :].rearrange("p (g e) -> p g e", g=KT),
                                          state[:, 4 * s + c, :].rearrange("p (g e) -> p g e", g=KT),
                                          gh[:, half, t, :, HD:2 * HD], ALU.add).then_inc(dve_own, 1)
                        own += 1
                        dve.wait_ge(dve_own, own)
                        dve.wait_ge(chain_mm, at(b, s, 4, c + 1))
                        dve.tensor_tensor(state[:, 4 * s + c + 1, :], s_plus[:, :], bank[4][:, P * c:P * c + P],
                                          ALU.subtract).then_inc(state_ready, 1)
                        if c == 0:
                            dve.wait_ge(gate_ready, at(b, s, 2, 2))
                        dve.wait_ge(o_mm, at(b, s, 4, c + 1))
                        i0 = P * t + C * half
                        dve.scalar_tensor_tensor(og[:, :, i0:i0 + C], gate[:, :, i0:i0 + C], 1.0,
                                                 bank[6 + half][:, C * KT * t:C * KT * t + C * KT].rearrange("p (g i) -> p g i", g=KT),
                                                 ALU.add, ALU.mult).then_inc(og_ready, 1)
                    dve.wait_ge(sq2_ready, at(b, s, TS, TS))
                    for g in range(KT):
                        dve.wait_ge(ro_ready, at(b, s, 2, g // 2 + 1))
                        dve.scalar_tensor_tensor(og[:, g, :], og[:, g, :], gnorm_half[:, g:g + 1], r_norm[:, g, :],
                                                 ALU.mult, ALU.mult).then_inc(ogn_ready, 1)
                    for t in range(TS):
                        dve.wait_ge(wo_mm, at(b, s, TS, t + 1))
                        dve.tensor_tensor(x_sp[:, s, t, :], x_sp[:, s, t, :], bank[1 + t][:, :], ALU.add).then_inc(x2_ready, 1)
                    dve.wait_ge(dve_own, own)
                    dve.sem_clear(dve_own)


NQ = 4
NKV = 8
DH = D // (NQ * NKV)
DKV = NKV * DH
NE, RANK = 8, 16
ER = NE * RANK
QUADS = NQ * NKV // 4
SR = 3 * DH + 1
LW = D // 2 + ER // 2 + NE
RW = D // 2 + ER // 2
SCORE_LAG, AV_LAG, OUT_LAG = 2, 3, 4


def token_layers(nc, dims, x2_in, w_ffn, b_ffn, lora_b, gate_b, w_q, w_kv, mem_aug_in, mem_w_in, ident_in, rank_mask_in, out):
    NBATCH, SEQ = dims
    NT = SEQ // P
    with ExitStack() as ctx:
        def sb(name, shape, dt=F32):
            return ctx.enter_context(nc.sbuf_tensor(name, shape, dt))

        def sem(name):
            return ctx.enter_context(nc.semaphore(name))

        ps = ctx.enter_context(nc.psum_tensor("row_psum", [P, 8, 512], F32))

        FW = LW + RW
        wf_hi = sb("wf_hi", [P, KT, FW], F32R)
        wf_lo = sb("wf_lo", [P, KT, FW], F32R)
        lb_hi = sb("lb_hi", [P, D], F32R)
        lb_lo = sb("lb_lo", [P, D], F32R)
        wq_hi = sb("wq_hi", [P, KT, D], F32R)
        wq_lo = sb("wq_lo", [P, KT, D], F32R)
        wkv_hi = sb("wkv_hi", [P, KT, 2 * DKV], F32R)
        wkv_lo = sb("wkv_lo", [P, KT, 2 * DKV], F32R)
        mem_aug = sb("mem_aug", [P, DKV + 1])
        mem_w = sb("mem_w", [P, 1])
        mem_wc = sb("mem_wc", [P, 1])
        bias_bc = sb("bias_bc", [P, D])
        gate_b_bc = sb("gate_b_bc", [P, NE])
        rank_mask = sb("rank_mask", [P, NE, NE])
        ident2 = sb("ident2", [P, P])
        minus_half = sb("minus_half4", [P, NT])
        ln_eps = sb("ln_eps4", [P, NT])

        xs = sb("xs", [P, 2, NT, D])
        stats = sb("stats4", [P, NT, 6])
        mv = sb("mv4", [P, NT, 2])
        var_eps = sb("var_eps4", [P, NT])
        rstd = sb("rstd4", [P, NT])
        x_hi = sb("xr_hi", [P, KT, SEQ], F32R)
        x_lo = sb("xr_lo", [P, KT, SEQ], F32R)
        lg = sb("lg", [P, NT, NE])
        lmax = sb("lmax", [P, NT])
        lp = sb("lp", [P, NT, NE])
        rank = sb("rank", [P, NT * NE])
        psum_g = sb("psum_g", [P, NT])
        xat_hi = sb("xat_hi", [P, SEQ], F32R)
        xat_lo = sb("xat_lo", [P, SEQ], F32R)
        q_stack = sb("q_stack", [P, NQ * NKV // 2, SEQ], F32R)
        k_stack = sb("k_stack", [P, NKV // 2, SEQ], F32R)
        v_aug = sb("v_aug", [P, NT, NKV, 32])
        smax = sb("smax", [P, NQ * NKV, NT])
        shift = sb("shift", [4, 2, SEQ], F32R)
        mem_rc = sb("mem_rc", [P, NT, NQ])
        av_sb = sb("av_sb", [P, 2, SEQ])
        av_rc = sb("av_rc", [P, NT, 4])
        av_n = sb("av_n", [P, NT, 4, DH])
        probs = sb("probs", [P, 2, 4, NT, SEQ])
        pool_mem = probs[:, :, :, :, :].rearrange("p a h t s -> p (a h t s)")

        def part(n, size):
            return pool_mem[:, n:n + size]
        xn = part(0, NT * D).rearrange("p (t d) -> p t d", t=NT)
        q_hi = part(2048, NQ * SEQ).rearrange("p (n s) -> p n s", n=NQ).bitcast(F32R)
        q_lo = part(4096, NQ * SEQ).rearrange("p (n s) -> p n s", n=NQ).bitcast(F32R)
        q_elu = part(6144, NQ * SEQ).rearrange("p (n s) -> p n s", n=NQ)
        q_exp = part(8192, NQ * SEQ).rearrange("p (n s) -> p n s", n=NQ)
        k_hi = part(10240, SEQ).bitcast(F32R)
        k_lo = part(10752, SEQ).bitcast(F32R)
        vT = part(11264, SEQ)
        a_mem = part(11776, NT * D).rearrange("p (t d) -> p t d", t=NT)
        cmp_gt = part(13824, NT * NE * NE).rearrange("p (t e j) -> p t e j", t=NT, e=NE)
        cmp_eq = part(14080, NT * NE * NE).rearrange("p (t e j) -> p t e j", t=NT, e=NE)
        xa = part(14336, NT * ER).rearrange("p (t r) -> p t r", t=NT)
        stage = part(0, KT * FW)

        w_in = sem("row_w_in"); w_hi_done = sem("row_w_hi"); w_lo_done = sem("row_w_lo"); c_in = sem("row_c_in")
        pool_consts = sem("row_pool_consts"); mem_tanh = sem("mem_tanh"); dve_consts = sem("row_dve_consts")
        x_loaded = [sem("row_x_loaded0"), sem("row_x_loaded1")]
        x_stored = sem("row_x_stored")
        var_ready = sem("row_var"); var_eps_ready = sem("row_var_eps"); rstd_ready = sem("row_rstd"); xn_ready = sem("row_xn"); bias_added = sem("bias_added")
        xT_ready = sem("row_xT"); xhi_ready = sem("row_xhi"); xlo_ready = sem("row_xlo")
        ffn_mm = sem("ffn_mm"); xa_ready = sem("xa_ready"); base_added = sem("base_added"); ldiff_ready = sem("ldiff_ready")
        lp_ready = sem("lp_ready"); xaw_ready = sem("xaw_ready"); xaT_mm = sem("xaT_mm"); xathi_ready = sem("xathi_ready")
        xatlo_ready = sem("xatlo_ready"); lora_mm = sem("lora_mm"); ffn_added = sem("ffn_added")
        q_mm = sem("q_mm"); qhi_ready = sem("row_qhi"); qexp_ready = sem("qexp_ready"); qlo_ready = sem("row_qlo"); qelu_ready = sem("qelu_ready")
        k_mm = sem("row_k_mm"); khi_ready = sem("row_khi"); klo_ready = sem("row_klo"); v_mm = sem("row_v_mm"); vT_ready = sem("vT_ready")
        vtok_mm = sem("vtok_mm"); v_ready = sem("row_v_ready"); stack_in = sem("stack_in")
        mem_mm = sem("mem_mm"); amem_ready = sem("amem_ready"); amem_added = sem("amem_added")
        max_mm = sem("max_mm"); max_ready = sem("max_ready"); maxT_mm = sem("maxT_mm"); shift_ready = sem("shift_ready"); shift_in = sem("shift_in")
        score_mm = sem("score_mm"); exp_ready = sem("exp_ready"); av_mm = sem("av_mm"); av_ready = sem("av_ready")
        avT_mm = sem("avT_mm"); adot_added = sem("adot_added"); dve_own = sem("row_dve_own")

        x2_rows = x2_in.rearrange("b (t p) d -> b p t d", p=P)
        out_rows = out.rearrange("b (t p) d -> b p t d", p=P)
        STORE_CREDIT = 48

        def at(b, per, k):
            return b * per + k

        def head(quad, i):
            return quad // 2, 4 * (quad % 2) + i

        block = ctx.enter_context(nc.Block())

        @block.sync
        def _(sp):
            sp.sem_inc(x_stored, STORE_CREDIT)
            for n, (src, size) in enumerate(((w_ffn, KT * FW), (lora_b, D), (w_q, KT * D), (w_kv, KT * 2 * DKV))):
                if n:
                    sp.wait_ge(w_lo_done, n)
                sp.dma_start(stage[:, 0:size], src).then_inc(w_in, 16)
            for dst, src in ((mem_aug, mem_aug_in), (mem_w, mem_w_in), (bias_bc, b_ffn), (gate_b_bc, gate_b),
                             (ident2, ident_in)):
                sp.dma_start(dst[:, :], src).then_inc(c_in, 16)
            sp.dma_start(rank_mask[:, :, :].rearrange("p e j -> p (e j)"), rank_mask_in).then_inc(c_in, 16)
            sp.dma_start(xs[:, 0, :, :], x2_rows[0]).then_inc(x_loaded[0], 16)
            sp.wait_ge(w_lo_done, 4)
            q_done, k_done = sp.alloc_register("q_done"), sp.alloc_register("k_done")
            with sp.Fori(0, NBATCH // 2) as bb:
                for par in range(2):
                    b = bb * 2 + par
                    if par == 0:
                        sp.wait_ge(x_stored, at(b, 16, STORE_CREDIT))
                        sp.dma_start(xs[:, 1, :, :], x2_rows[bb * 2 + 1]).then_inc(x_loaded[1], 16)
                    sp.reg_mov(q_done, at(b, NQ, NQ))
                    sp.reg_mov(k_done, at(b, 1, 1))
                    sp.wait_ge(qhi_ready, q_done)
                    sp.wait_ge(qlo_ready, q_done)
                    sp.wait_ge(khi_ready, k_done)
                    sp.wait_ge(klo_ready, k_done)
                    for h in range(NKV):
                        rows = slice(DH * h, DH * h + DH)
                        for n, (q_part, k_part) in enumerate(((q_hi, k_hi), (q_lo, k_hi), (q_hi, k_lo))):
                            r0 = 64 * (h % 2) + DH * n
                            sp.dma_start(k_stack[r0:r0 + DH, h // 2, :].bitcast(F32), k_part[rows, :].bitcast(F32)).then_inc(stack_in, 16)
                            sp.dma_start(q_stack[r0:r0 + DH, h // 2:NQ * NKV // 2:NKV // 2, :].bitcast(F32),
                                         q_part[rows, :, :].bitcast(F32)).then_inc(stack_in, 16)
                    for quad in range(QUADS):
                        sp.wait_ge(shift_ready, at(b, QUADS, quad + 1))
                        for i in range(4):
                            n, h = head(quad, i)
                            r0 = 64 * (h % 2) + 3 * DH
                            sp.dma_start(q_stack[r0:r0 + 1, n * (NKV // 2) + h // 2, :].bitcast(F32),
                                         shift[i:i + 1, quad % 2, :].bitcast(F32)).then_inc(shift_in, 16)
                    sp.wait_ge(ffn_added, at(b, 2 * NT, 2 * NT))
                    sp.dma_start(out_rows[b], xs[:, par, :, :]).then_inc(x_stored, 16)
                    if par == 1:
                        sp.wait_ge(x_stored, at(b, 16, STORE_CREDIT))
                        sp.dma_start(xs[:, 0, :, :], x2_rows[(bb * 2 + 2) % NBATCH]).then_inc(x_loaded[0], 16)
            sp.wait_ge(x_stored, STORE_CREDIT + NBATCH * 16)
            sp.wait_ge(x_loaded[0], 16 * (NBATCH // 2 + 1))

        @block.gpsimd
        def _(pool):
            pool.memset(minus_half[:, :], -0.5).then_inc(pool_consts, 1)
            pool.memset(ln_eps[:, :], LN_EPS).then_inc(pool_consts, 1)
            pool.memset(v_aug[:, :, :, :], 1.0).then_inc(pool_consts, 1)
            pool.memset(k_stack[:, :, :].bitcast(F32), 1.0).then_inc(pool_consts, 1)
            pool.wait_ge(pool_consts, 4)
            pool.wait_ge(c_in, 96)
            with pool.Fori(0, NBATCH // 2) as bb:
                for par in range(2):
                    b = bb * 2 + par

                    def layer_norm(f):
                        pool.wait_ge(var_ready, at(b, 3 * NT, NT * (f + 1)))
                        pool.tensor_tensor(var_eps[:, :], mv[:, :, 1], ln_eps[:, :], ALU.add).then_inc(var_eps_ready, 1)
                        pool.wait_ge(var_eps_ready, at(b, 3, f + 1))
                        pool.tensor_tensor(rstd[:, :], var_eps[:, :], minus_half[:, :], ALU.pow).then_inc(rstd_ready, 1)

                    def ffn(f):
                        pool.wait_ge(xn_ready, at(b, 3 * NT, NT * (2 * f + 1)))
                        for t in range(NT):
                            pool.tensor_tensor(xs[:, par, t, :], xs[:, par, t, :], bias_bc[:, :], ALU.add).then_inc(bias_added, 1)

                    layer_norm(0)
                    ffn(0)
                    layer_norm(1)
                    for t in range(NT):
                        pool.wait_ge(amem_ready, at(b, NT, t + 1))
                        pool.tensor_tensor(xs[:, par, t, :], xs[:, par, t, :], a_mem[:, t, :], ALU.add).then_inc(amem_added, 1)
                    layer_norm(2)
                    ffn(1)

        @block.scalar
        def _(act):
            for n, (dst, size) in enumerate(((wf_hi, KT * FW), (lb_hi, D), (wq_hi, KT * D), (wkv_hi, KT * 2 * DKV))):
                act.wait_ge(w_in, 16 * (n + 1))
                d2 = dst[:, :] if n == 1 else dst[:, :, :].rearrange("p k n -> p (k n)")
                act.activation(d2, stage[:, 0:size], ACT.Copy).then_inc(w_hi_done, 1)
            act.wait_ge(c_in, 96)
            act.activation(mem_w[:, :], mem_w[:, :], ACT.Tanh, scale=0.5).then_inc(mem_tanh, 1)
            with act.Fori(0, NBATCH // 2) as bb:
                for par in range(2):
                    b = bb * 2 + par

                    def norm_hi(f):
                        for k in range(KT):
                            act.wait_ge(xT_ready, at(b, 3 * KT, KT * f + k + 1))
                            act.activation(x_hi[:, k, :], ps[:, k, :], ACT.Copy).then_inc(xhi_ready, 1)

                    def ffn(f):
                        norm_hi(2 * f)
                        for t in range(NT):
                            left = 4 + 2 * (t % 2)
                            act.wait_ge(ffn_mm, at(b, 2 * NT, NT * f + t + 1))
                            act.activation(xa[:, t, :].rearrange("p (c r) -> p c r", c=2), ps[:, left:left + 2, D // 2:D // 2 + ER // 2],
                                           ACT.Copy).then_inc(xa_ready, 1)
                        act.wait_ge(ldiff_ready, at(b, 2, f + 1))
                        act.activation(lp[:, :, :], lp[:, :, :], ACT.Exp).then_inc(lp_ready, 1)
                        act.wait_ge(xaT_mm, at(b, 2, f + 1))
                        act.activation(xat_hi[:, :], ps[:, 0, :], ACT.Copy).then_inc(xathi_ready, 1)

                    ffn(0)
                    norm_hi(1)
                    for n in range(NQ):
                        act.wait_ge(q_mm, at(b, NQ, n + 1))
                        act.activation(q_hi[:, n, :], ps[:, 4 + n, :], ACT.Copy).then_inc(qhi_ready, 1)
                        act.activation(q_exp[:, n, :], ps[:, 4 + n, :], ACT.Exp).then_inc(qexp_ready, 1)
                    act.wait_ge(k_mm, at(b, 1, 1))
                    act.activation(k_hi, ps[:, 0, :], ACT.Copy).then_inc(khi_ready, 1)
                    act.wait_ge(v_mm, at(b, 1, 1))
                    act.activation(vT, ps[:, 1, :], ACT.Copy).then_inc(vT_ready, 1)
                    act.wait_ge(stack_in, at(b, 16 * 6 * NKV, 16 * 6 * NKV))
                    act.wait_ge(amem_added, at(b, NT, NT))
                    act.wait_ge(vtok_mm, at(b, 1, 1))
                    for step in range(QUADS + OUT_LAG):
                        for i in range(4):
                            quad = step - SCORE_LAG
                            if 0 <= quad < QUADS:
                                for j in range(2):
                                    act.wait_ge(score_mm, at(b, 8 * QUADS, 8 * quad + 2 * i + j + 1))
                                    if quad >= 2 and i == 0 and j == 0:
                                        act.wait_ge(av_mm, at(b, QUADS, quad - 1))
                                    act.activation(probs[:, quad % 2, i, 2 * j:2 * j + 2, :], ps[:, 2 * j:2 * j + 2, :], ACT.Exp,
                                                   scale=float(DH) ** -0.5).then_inc(exp_ready, 1)
                            quad = step - AV_LAG
                            if i == 3 and 0 <= quad < QUADS:
                                act.wait_ge(av_mm, at(b, QUADS, quad + 1))
                                if quad >= 2:
                                    act.wait_ge(avT_mm, at(b, QUADS, quad - 1))
                                act.activation(av_sb[:, quad % 2, :], ps[:, 6, :], ACT.Copy).then_inc(av_ready, 1)
                    ffn(1)

        @block.tensor
        def _(pe):
            pe.wait_ge(w_lo_done, 4)
            pe.wait_ge(w_hi_done, 4)
            pe.wait_ge(c_in, 96)
            pe.wait_ge(pool_consts, 4)
            with pe.Fori(0, NBATCH // 2) as bb:
                for par in range(2):
                    b = bb * 2 + par

                    def turned(f):
                        pe.wait_ge(xn_ready, at(b, 3 * NT, NT * (f + 1)))
                        for k in range(KT):
                            for t in range(NT):
                                last = pe.transpose(ps[:, k, P * t:P * t + P], xn[:, t, P * k:P * k + P], ident2[:, :])
                            last.then_inc(xT_ready, 1)
                        pe.wait_ge(xhi_ready, at(b, 3 * KT, KT * (f + 1)))
                        pe.wait_ge(xlo_ready, at(b, 3 * KT, KT * (f + 1)))

                    def ffn(f):
                        turned(2 * f)
                        for t in range(NT):
                            left = 4 + 2 * (t % 2)
                            if t >= 2:
                                pe.wait_ge(xa_ready, at(b, 2 * NT, NT * f + t - 1))
                                pe.wait_ge(base_added, at(b, 2 * NT, NT * f + t - 1))
                            tok = slice(P * t, P * t + P)
                            for k in range(KT):
                                split3(pe, ps[:, left, 0:LW], x_hi[:, k, tok], x_lo[:, k, tok],
                                       wf_hi[:, k, 0:LW], wf_lo[:, k, 0:LW], k == 0, k == KT - 1)
                            for k in range(KT):
                                last = split3(pe, ps[:, left + 1, 0:RW], x_hi[:, k, tok], x_lo[:, k, tok],
                                              wf_hi[:, k, LW:FW], wf_lo[:, k, LW:FW], k == 0, k == KT - 1)
                            last.then_inc(ffn_mm, 1)
                        pe.wait_ge(xaw_ready, at(b, 2, f + 1))
                        for t in range(NT):
                            last = pe.transpose(ps[:, 0, P * t:P * t + P], xa[:, t, :], ident2[:, :])
                        last.then_inc(xaT_mm, 1)
                        pe.wait_ge(xathi_ready, at(b, 2, f + 1))
                        pe.wait_ge(xatlo_ready, at(b, 2, f + 1))
                        for t in range(NT):
                            tok = slice(P * t, P * t + P)
                            split3(pe, ps[:, 4 + t, :], xat_hi[:, tok], xat_lo[:, tok], lb_hi[:, :], lb_lo[:, :],
                                   True, True).then_inc(lora_mm, 1)

                    ffn(0)
                    turned(1)
                    for n in range(NQ):
                        if n == 0:
                            pe.wait_ge(ffn_added, at(b, 2 * NT, NT))
                        for k in range(KT):
                            last = split3(pe, ps[:, 4 + n, :], wq_hi[:, k, P * n:P * n + P], wq_lo[:, k, P * n:P * n + P],
                                          x_hi[:, k, :], x_lo[:, k, :], k == 0, k == KT - 1)
                        last.then_inc(q_mm, 1)
                    for n, done in ((0, k_mm), (1, v_mm)):
                        for k in range(KT):
                            last = split3(pe, ps[:, n, :], wkv_hi[:, k, DKV * n:DKV * n + DKV], wkv_lo[:, k, DKV * n:DKV * n + DKV],
                                          x_hi[:, k, :], x_lo[:, k, :], k == 0, k == KT - 1)
                        last.then_inc(done, 1)
                    pe.wait_ge(vT_ready, at(b, 1, 1))
                    for t in range(NT):
                        last = pe.transpose(ps[:, 2, P * t:P * t + P], vT[:, P * t:P * t + P], ident2[:, :])
                    last.then_inc(vtok_mm, 1)
                    for t in range(NT):
                        if t == 0:
                            pe.wait_ge(qelu_ready, at(b, NQ, NQ))
                            pe.wait_ge(qlo_ready, at(b, NQ, NQ))
                        if t >= 2:
                            pe.wait_ge(amem_ready, at(b, NT, t - 1))
                        for n in range(NQ):
                            c0 = (DKV + 1) * (n % 2)
                            last = pe.matmul(ps[:, 4 + 2 * (t % 2) + n // 2, c0:c0 + DKV + 1], q_elu[:, n, P * t:P * t + P],
                                             mem_aug[:, :], start=True, stop=True)
                        last.then_inc(mem_mm, 1)

                    pe.wait_ge(stack_in, at(b, 16 * 6 * NKV, 16 * 6 * NKV))
                    pe.wait_ge(v_ready, at(b, 1, 1))
                    pe.wait_ge(klo_ready, at(b, 1, 1))
                    pe.wait_ge(amem_ready, at(b, NT, NT))

                    def stack(ap, quad, i, rows):
                        n, h = head(quad, i)
                        r0 = 64 * (h % 2)
                        return ap[r0:r0 + rows, (n * (NKV // 2) if ap is q_stack else 0) + h // 2, :]

                    for step in range(QUADS + OUT_LAG):
                        for i in range(4):
                            quad = step
                            if quad < QUADS:
                                for j in range(2):
                                    for st in (2 * j, 2 * j + 1):
                                        m = 16 * quad + 4 * i + st
                                        if m >= 2:
                                            pe.wait_ge(max_ready, at(b, 16 * QUADS, m - 1))
                                        pe.matmul(ps[:, 4 + st % 2, :], stack(q_stack, quad, i, SR - 1)[:, P * st:P * st + P],
                                                  stack(k_stack, quad, i, SR - 1), start=True, stop=True).then_inc(max_mm, 1)
                            quad = step - 1
                            if i == 1 and 0 <= quad < QUADS:
                                pe.wait_ge(max_ready, at(b, 16 * QUADS, 16 * quad + 16))
                                if quad:
                                    pe.wait_ge(shift_ready, at(b, QUADS, quad))
                                if quad >= OUT_LAG:
                                    pe.wait_ge(adot_added, at(b, QUADS, quad - OUT_LAG + 1))
                                for st in range(NT):
                                    last = pe.transpose(ps[0:4, 7, P * st:P * st + P], smax[:, 4 * quad:4 * quad + 4, st], ident2[:, :])
                                last.then_inc(maxT_mm, 1)
                            quad = step - SCORE_LAG
                            if 0 <= quad < QUADS:
                                if i == 0:
                                    pe.wait_ge(shift_in, at(b, 64 * QUADS, 64 * (quad + 1)))
                                for tt in range(NT):
                                    j = tt // 2
                                    if tt % 2 == 0 and (quad or i):
                                        pe.wait_ge(exp_ready, at(b, 8 * QUADS, 8 * quad + 2 * i + j - 1))
                                    last = pe.matmul(ps[:, tt, :], stack(k_stack, quad, i, SR)[:, P * tt:P * tt + P],
                                                     stack(q_stack, quad, i, SR), start=True, stop=True)
                                    if tt % 2:
                                        last.then_inc(score_mm, 1)
                            quad = step - AV_LAG
                            if i == 2 and 0 <= quad < QUADS:
                                pe.wait_ge(exp_ready, at(b, 8 * QUADS, 8 * quad + 8))
                                if quad:
                                    pe.wait_ge(av_ready, at(b, QUADS, quad))
                                for tt in range(NT):
                                    for e in range(4):
                                        h = head(quad, e)[1]
                                        last = pe.matmul(ps[32 * e:32 * e + 32, 6, :], v_aug[:, tt, h, :], probs[:, quad % 2, e, tt, :],
                                                         start=tt == 0, stop=tt == NT - 1)
                                last.then_inc(av_mm, 1)
                            quad = step - OUT_LAG
                            if i == 2 and 0 <= quad < QUADS:
                                pe.wait_ge(av_ready, at(b, QUADS, quad + 1))
                                pe.wait_ge(shift_ready, at(b, QUADS, min(quad + OUT_LAG, QUADS)))
                                if quad:
                                    pe.wait_ge(adot_added, at(b, QUADS, quad))
                                for t in range(NT):
                                    last = pe.transpose(ps[:, 7, P * t:P * t + P], av_sb[:, quad % 2, P * t:P * t + P], ident2[:, :])
                                last.then_inc(avT_mm, 1)
                    ffn(1)

        @block.vector
        def _(dve):
            for n, (lo, hi, size) in enumerate(((wf_lo, wf_hi, KT * FW), (lb_lo, lb_hi, D), (wq_lo, wq_hi, KT * D),
                                                (wkv_lo, wkv_hi, KT * 2 * DKV))):
                dve.wait_ge(w_hi_done, n + 1)
                flat = (lambda a: a[:, :]) if n == 1 else (lambda a: a[:, :, :].rearrange("p k n -> p (k n)"))
                dve.tensor_tensor(flat(lo), stage[:, 0:size], flat(hi).bitcast(F32), ALU.subtract).then_inc(w_lo_done, 1)
            dve.wait_ge(mem_tanh, 1)
            dve.tensor_scalar(mem_wc[:, :], mem_w[:, :], -0.5, 0.5, ALU.mult, ALU.add).then_inc(dve_consts, 1)
            dve.wait_ge(dve_consts, 1)
            dve.tensor_scalar(mem_w[:, :], mem_w[:, :], 0.5, 0.5, ALU.mult, ALU.add).then_inc(dve_consts, 1)
            dve.wait_ge(dve_consts, 2)
            dve.wait_ge(c_in, 96)
            dve.wait_ge(pool_consts, 4)
            with dve.Fori(0, NBATCH // 2) as bb:
                for par in range(2):
                    b = bb * 2 + par
                    own = [0]

                    def mark(ins):
                        own[0] += 1
                        ins.then_inc(dve_own, 1)

                    def layer_norm(f):
                        for t in range(NT):
                            mark(dve.bn_stats(stats[:, t, :], xs[:, par, t, :]))
                        for t in range(NT):
                            dve.wait_ge(dve_own, own[0] - NT + 1 + t)
                            dve.bn_aggr(mv[:, t, :], stats[:, t, :]).then_inc(var_ready, 1)
                        dve.wait_ge(var_ready, at(b, 3 * NT, NT * (f + 1)))
                        dve.wait_ge(rstd_ready, at(b, 3, f + 1))
                        for t in range(NT):
                            dve.tensor_scalar(xn[:, t, :], xs[:, par, t, :], mv[:, t, 0:1], rstd[:, t:t + 1],
                                              ALU.subtract, ALU.mult).then_inc(xn_ready, 1)
                        for k in range(KT):
                            dve.wait_ge(xhi_ready, at(b, 3 * KT, KT * f + k + 1))
                            dve.tensor_tensor(x_lo[:, k, :], ps[:, k, :], x_hi[:, k, :].bitcast(F32), ALU.subtract).then_inc(xlo_ready, 1)

                    def ffn(f):
                        layer_norm(2 * f)
                        dve.wait_ge(bias_added, at(b, 2 * NT, NT * (f + 1)))
                        for t in range(NT):
                            left = 4 + 2 * (t % 2)
                            dve.wait_ge(ffn_mm, at(b, 2 * NT, NT * f + t + 1))
                            dve.wait_ge(xa_ready, at(b, 2 * NT, NT * f + t + 1))
                            mark(dve.tensor_tensor(lg[:, t, :], ps[:, left, LW - NE:LW], gate_b_bc[:, :], ALU.add))
                            x2 = xs[:, par, t, :].rearrange("p (c d) -> p c d", c=2)
                            dve.tensor_tensor(x2, x2, ps[:, left:left + 2, 0:D // 2], ALU.add).then_inc(base_added, 1)
                        dve.wait_ge(dve_own, own[0])
                        mark(dve.tensor_reduce(lmax[:, :], lg[:, :, :], AX.X, ALU.max))
                        l_e = lg[:, :, :].rearrange("p t (e o) -> p t e o", o=1).to_broadcast([P, NT, NE, NE])
                        l_j = lg[:, :, :].rearrange("p t (o j) -> p t o j", o=1).to_broadcast([P, NT, NE, NE])
                        mark(dve.tensor_tensor(cmp_gt[:, :, :, :], l_j, l_e, ALU.is_gt))
                        mark(dve.tensor_tensor(cmp_eq[:, :, :, :], l_j, l_e, ALU.is_equal))
                        dve.wait_ge(dve_own, own[0] - 2)
                        dve.tensor_tensor(lp[:, :, :], lg[:, :, :],
                                          lmax[:, :].rearrange("p (t o) -> p t o", o=1).to_broadcast([P, NT, NE]),
                                          ALU.subtract).then_inc(ldiff_ready, 1)
                        dve.wait_ge(dve_own, own[0])
                        mark(dve.tensor_tensor(cmp_eq[:, :, :, :], cmp_eq[:, :, :, :],
                                               rank_mask[:, :, :].rearrange("p (o e) j -> p o e j", o=1).to_broadcast([P, NT, NE, NE]),
                                               ALU.mult))
                        dve.wait_ge(dve_own, own[0])
                        mark(dve.tensor_tensor(cmp_gt[:, :, :, :], cmp_gt[:, :, :, :], cmp_eq[:, :, :, :], ALU.add))
                        dve.wait_ge(dve_own, own[0])
                        mark(dve.tensor_reduce(rank[:, :], cmp_gt[:, :, :, :].rearrange("p t e j -> p (t e) j"), AX.X, ALU.add))
                        dve.wait_ge(dve_own, own[0])
                        dve.wait_ge(lp_ready, at(b, 2, f + 1))
                        lp2 = lp[:, :, :].rearrange("p t e -> p (t e)")
                        mark(dve.scalar_tensor_tensor(lp2, rank[:, :], 2.0, lp2, ALU.is_lt, ALU.mult))
                        dve.wait_ge(dve_own, own[0])
                        mark(dve.tensor_reduce(psum_g[:, :], lp[:, :, :], AX.X, ALU.add))
                        dve.wait_ge(dve_own, own[0])
                        mark(dve.reciprocal(psum_g[:, :], psum_g[:, :]))
                        dve.wait_ge(dve_own, own[0])
                        mark(dve.tensor_tensor(lp[:, :, :], lp[:, :, :],
                                               psum_g[:, :].rearrange("p (t o) -> p t o", o=1).to_broadcast([P, NT, NE]), ALU.mult))
                        dve.wait_ge(dve_own, own[0])
                        xa3 = xa[:, :, :].rearrange("p t (e r) -> p (t e) r", e=NE)
                        dve.tensor_tensor(xa3, xa3, lp2.rearrange("p (e o) -> p e o", o=1).to_broadcast([P, NT * NE, RANK]),
                                          ALU.mult).then_inc(xaw_ready, 1)
                        dve.wait_ge(xathi_ready, at(b, 2, f + 1))
                        dve.tensor_tensor(xat_lo[:, :], ps[:, 0, :], xat_hi[:, :].bitcast(F32), ALU.subtract).then_inc(xatlo_ready, 1)
                        dve.wait_ge(base_added, at(b, 2 * NT, NT * (f + 1)))
                        for t in range(NT):
                            dve.wait_ge(lora_mm, at(b, 2 * NT, NT * f + t + 1))
                            dve.tensor_tensor(xs[:, par, t, :], xs[:, par, t, :], ps[:, 4 + t, :], ALU.add).then_inc(ffn_added, 1)

                    dve.wait_ge(x_loaded[par], bb * 16 + 16)
                    ffn(0)
                    dve.wait_ge(ffn_added, at(b, 2 * NT, NT))
                    layer_norm(1)
                    for n in range(NQ):
                        dve.wait_ge(qexp_ready, at(b, NQ, n + 1))
                        dve.tensor_tensor(q_lo[:, n, :], ps[:, 4 + n, :], q_hi[:, n, :].bitcast(F32), ALU.subtract).then_inc(qlo_ready, 1)
                        mark(dve.tensor_scalar(q_exp[:, n, :], q_exp[:, n, :], 1.0, -1.0, ALU.min, ALU.add))
                        dve.wait_ge(dve_own, own[0])
                        dve.scalar_tensor_tensor(q_elu[:, n, :], ps[:, 4 + n, :], 0.0, q_exp[:, n, :], ALU.max, ALU.add).then_inc(qelu_ready, 1)
                    dve.wait_ge(khi_ready, at(b, 1, 1))
                    dve.tensor_tensor(k_lo, ps[:, 0, :], k_hi.bitcast(F32), ALU.subtract).then_inc(klo_ready, 1)
                    dve.wait_ge(vtok_mm, at(b, 1, 1))
                    dve.tensor_scalar(v_aug[:, :, :, 0:DH], ps[:, 2, :].rearrange("p (t h e) -> p t h e", t=NT, h=NKV),
                                      mem_wc[:, 0:1], None, ALU.mult).then_inc(v_ready, 1)
                    for t in range(NT):
                        dve.wait_ge(mem_mm, at(b, NT, t + 1))
                        pv = ps[:, 4 + 2 * (t % 2):6 + 2 * (t % 2), 0:2 * (DKV + 1)].rearrange("p c (n e) -> p c n e", n=2)
                        rc = mem_rc[:, t, :].rearrange("p (c n) -> p c n", c=2)
                        mark(dve.reciprocal(rc, pv[:, :, :, DKV]))
                        dve.wait_ge(dve_own, own[0])
                        mark(dve.tensor_scalar(rc, rc, mem_w[:, 0:1], None, ALU.mult))
                        dve.wait_ge(dve_own, own[0])
                        for c in range(2):
                            last = dve.tensor_tensor(a_mem[:, t, 2 * DKV * c:2 * DKV * c + 2 * DKV].rearrange("p (n e) -> p n e", n=2),
                                                     pv[:, c, :, 0:DKV],
                                                     rc[:, c, :].rearrange("p (n o) -> p n o", o=1).to_broadcast([P, 2, DKV]), ALU.mult)
                        last.then_inc(amem_ready, 1)
                    for step in range(QUADS + OUT_LAG + 1):
                        for i in range(4):
                            quad = step
                            if quad < QUADS:
                                for st in range(NT):
                                    dve.wait_ge(max_mm, at(b, 16 * QUADS, 16 * quad + 4 * i + st + 1))
                                    dve.tensor_reduce(smax[:, 4 * quad + i, st:st + 1], ps[:, 4 + st % 2, :], AX.X, ALU.max).then_inc(max_ready, 1)
                            quad = step - 1
                            if i == 2 and 0 <= quad < QUADS:
                                dve.wait_ge(maxT_mm, at(b, QUADS, quad + 1))
                                if quad >= 2:
                                    dve.wait_ge(shift_in, at(b, 64 * QUADS, 64 * (quad - 1)))
                                dve.tensor_scalar(shift[:, quad % 2, :], ps[0:4, 7, :], -1.0, None, ALU.mult).then_inc(shift_ready, 1)
                            quad = step - OUT_LAG
                            if i == 3 and 0 <= quad < QUADS:
                                dve.wait_ge(avT_mm, at(b, QUADS, quad + 1))
                                pv = ps[:, 7, :].rearrange("p (t h e) -> p t h e", t=NT, h=4)
                                mark(dve.reciprocal(av_rc[:, :, :], pv[:, :, :, DH]))
                                dve.wait_ge(dve_own, own[0])
                                mark(dve.tensor_tensor(av_n[:, :, :, :], pv[:, :, :, 0:DH],
                                                       av_rc[:, :, :].rearrange("p t (h o) -> p t h o", o=1).to_broadcast([P, NT, 4, DH]), ALU.mult))
                                dve.wait_ge(dve_own, own[0])
                                if quad == 0:
                                    dve.wait_ge(amem_added, at(b, NT, NT))
                                xq = xs[:, par, :, 64 * quad:64 * quad + 64]
                                dve.tensor_tensor(xq, xq, av_n[:, :, :, :].rearrange("p t h e -> p t (h e)"), ALU.add).then_inc(adot_added, 1)
                    dve.wait_ge(adot_added, at(b, QUADS, QUADS))
                    ffn(1)
                    dve.wait_ge(dve_own, own[0])
                    dve.sem_clear(dve_own)


def kernel(L0_attn_a_x, L0_attn_a_Wq, L0_attn_a_Wk, L0_attn_a_Wv, L0_attn_a_Wbeta, L0_attn_a_Wg1, L0_attn_a_Wg2, L0_attn_a_g_norm,
           L0_attn_a_Wo, L0_attn_b_Wq, L0_attn_b_Wk, L0_attn_b_Wv, L0_attn_b_memory, L0_attn_b_memory_norm, L0_attn_b_memory_weight,
           L0_ffn_W, L0_ffn_b, L0_ffn_lora_A, L0_ffn_lora_B, L0_ffn_gate_w, L0_ffn_gate_b):
    import numpy as np
    import concourse.bacc as bacc
    from concourse.bass_utils import run_bass_kernel_spmd

    def by_input(w):
        w = np.asarray(w)
        o, d = w.shape
        return np.ascontiguousarray(w.T.reshape(d // P, P, o).transpose(1, 0, 2).reshape(P, -1))

    def on_all(v):
        v = np.asarray(v).reshape(1, -1)
        return np.ascontiguousarray(np.broadcast_to(v, (P, v.shape[1])))

    j = np.arange(C)
    causal = np.concatenate([j[:, None] < j[None, :], j[:, None] <= j[None, :]], 1).astype(np.float32)
    e = np.arange(NE)
    x = np.ascontiguousarray(np.asarray(L0_attn_a_x))
    w_f, lora_a, gate_w = np.asarray(L0_ffn_W), np.asarray(L0_ffn_lora_A).reshape(ER, D), np.asarray(L0_ffn_gate_w)
    arrays = {
        "in_x": x,
        "in_w_main": np.stack([by_input(w) for w in (L0_attn_a_Wk, L0_attn_a_Wq, L0_attn_a_Wv, L0_attn_a_Wo)]),
        "in_w_gb": by_input(np.concatenate([np.asarray(L0_attn_a_Wg1)] * 3 + [np.asarray(L0_attn_a_Wbeta)], 0)),
        "in_w_g2": np.concatenate([np.asarray(L0_attn_a_Wg2).T] * 3, 0),
        "in_g_norm": np.ascontiguousarray(np.asarray(L0_attn_a_g_norm).reshape(KT, P).T),
        "in_ident": np.eye(P, dtype=np.float32),
        "in_masks": np.concatenate([causal, causal], 0),
        "in_head_ones": np.kron(np.eye(HPT), np.ones((HD, HD))).astype(np.float32),
        "in_w_ffn": by_input(np.concatenate([w_f[:D // 2], lora_a[:ER // 2], gate_w, w_f[D // 2:], lora_a[ER // 2:]], 0)),
        "in_b_ffn": on_all(L0_ffn_b),
        "in_lora_b": np.ascontiguousarray(np.asarray(L0_ffn_lora_B).transpose(0, 2, 1).reshape(ER, D)),
        "in_gate_b": on_all(L0_ffn_gate_b),
        "in_w_q": by_input(L0_attn_b_Wq),
        "in_w_kv": by_input(np.concatenate([np.asarray(L0_attn_b_Wk), np.asarray(L0_attn_b_Wv)], 0)),
        "in_mem_aug": np.concatenate([np.asarray(L0_attn_b_memory), np.asarray(L0_attn_b_memory_norm)], 1),
        "in_mem_w": on_all(L0_attn_b_memory_weight),
        "in_rank_mask": on_all(e[None, :] < e[:, None]).astype(np.float32),
    }
    arrays = {k: np.ascontiguousarray(v) for k, v in arrays.items()}

    nc = bacc.Bacc("TRN2", target_bir_lowering=False, num_devices=1)
    a = {k: nc.dram_tensor(k, v.shape, mybir.dt.from_np(v.dtype), kind="ExternalInput").ap() for k, v in arrays.items()}
    out = nc.dram_tensor("y", x.shape, F32, kind="ExternalOutput").ap()
    x2 = nc.dram_tensor("x2", x.shape, F32, kind="Internal").ap()
    dims = x.shape[:2]
    delta_rule_layer(nc, dims, a["in_x"], a["in_w_main"], a["in_w_gb"], a["in_w_g2"], a["in_g_norm"], a["in_ident"],
                     a["in_masks"], a["in_head_ones"], x2)
    token_layers(nc, dims, x2, a["in_w_ffn"], a["in_b_ffn"], a["in_lora_b"], a["in_gate_b"], a["in_w_q"], a["in_w_kv"],
                 a["in_mem_aug"], a["in_mem_w"], a["in_ident"], a["in_rank_mask"], out)
    r = run_bass_kernel_spmd(nc, [arrays], core_ids=[0])
    return r.results[0]["y"]
```

```python
from contextlib import ExitStack

import concourse.bass as bass
from concourse import mybir

F32 = mybir.dt.float32
F32R = mybir.dt.float32r
ALU = mybir.AluOpType
ACT = mybir.ActivationFunctionType
AX = mybir.AxisListType

P = 128
KT = 4
D = P * KT
H = 16
HD = D // H
HPT = P // HD
SPAN = 256
TS = SPAN // P
C = 64
NB = 32
LN_EPS = 1e-5
EPS = 1e-6


def split3(pe, out, a_hi, a_lo, b_hi, b_lo, first, last):
    pe.matmul(out, a_hi, b_hi, start=first, stop=False)
    pe.matmul(out, a_hi, b_lo, start=False, stop=False)
    return pe.matmul(out, a_lo, b_hi, start=False, stop=last)


def delta_rule_layer(nc, dims, x_in, w_main, w_gb, w_g2, g_norm, ident_in, masks_in, ones_in, out):
    NBATCH, SEQ = dims
    SPB = SEQ // SPAN

    tri_dram = nc.dram_tensor("tri_dram", [TS * 4, H, NB, NB], F32, kind="Internal").ap()
    beta_dram = nc.dram_tensor("beta_dram", [TS * 4, H, NB], F32, kind="Internal").ap()
    inv_dram = nc.dram_tensor("inv_dram", [TS * 4, H, NB, NB], F32, kind="Internal").ap()

    with ExitStack() as ctx:
        def sb(name, shape, dt=F32):
            return ctx.enter_context(nc.sbuf_tensor(name, shape, dt))

        def sem(name):
            return ctx.enter_context(nc.semaphore(name))

        bank = [ctx.enter_context(nc.psum_tensor(f"span_bank{n}", [P, 512], F32)) for n in range(8)]

        NW = 4
        w_hi = sb("w_hi", [P, NW, KT, D], F32R)
        w_lo = sb("w_lo", [P, NW, KT, D], F32R)
        gb_hi = sb("gb_hi", [P, KT, HD + H], F32R)
        gb_lo = sb("gb_lo", [P, KT, HD + H], F32R)
        g2 = sb("g2", [HD, D])
        gnorm_half = sb("gnorm_half", [P, KT])
        ident = sb("ident", [P, P])
        masks = sb("masks", [P, 2 * C])
        head_ones = sb("head_ones", [P, P])
        eps_t = sb("eps_t", [P, 1])
        minus_half = sb("minus_half", [P, TS])
        ln_eps = sb("ln_eps", [P, TS])

        x_sp = sb("x_sp", [P, TS, D])
        x_res = sb("x_res", [P, TS, D])
        stats = sb("stats", [P, TS, 6])
        mv = sb("mv", [P, TS, 2])
        var_eps = sb("var_eps", [P, TS])
        rstd = sb("rstd", [P, TS])
        x_hi = sb("x_hi", [P, KT, SPAN], F32R)
        x_lo = sb("x_lo", [P, KT, SPAN], F32R)
        sq = sb("sq", [P, KT, SPAN])
        r_norm = sb("r_norm", [P, KT, SPAN])
        xn = r_norm[:, :, :].rearrange("p g i -> p (g i)").rearrange("p (t d) -> p t d", t=TS)
        kq = sb("kq", [P, KT, 1 + SPB, SPAN])
        g1_beta = sb("g1_beta", [HD + H, SPAN])
        g1, beta_t = g1_beta[0:HD, :], g1_beta[HD:HD + H, :]
        gate = sb("gate", [P, SPB, KT, SPAN])
        rhs = sb("rhs", [P, SPB, TS, H, 2 * HD])
        tri = sb("tri", [P, SPB, TS, KT, HPT, 2 * C])
        stage = tri[:, 0, :, :, :, :].rearrange("p t g e i -> p (t g e i)")[:, 0:KT * D]
        lane_t = sb("lane_t", [P, NB, NB])
        lane_b = sb("lane_b", [P, NB])
        lane_p = sb("lane_p", [P, NB // 2 * (NB // 2 - 1)])
        inv_b = sb("inv_b", [P, TS, H, NB])
        uw = sb("uw", [P, TS, H, 2 * HD])
        rhs2 = sb("rhs2", [P, TS, H, 2 * HD])
        gh = sb("gh", [P, 2, TS, KT, 2 * HD])
        state = sb("state", [P, SPB * 4 + 1, KT * HD])
        og = sb("og", [P, KT, SPAN])
        o_hi = sb("o_hi", [P, KT, SPAN], F32R)
        o_lo = sb("o_lo", [P, KT, SPAN], F32R)

        w_in = sem("w_in"); w_split = sem("w_split"); c_in = sem("c_in"); pool_consts = sem("pool_consts"); dve_consts = sem("dve_consts")
        x_loaded = sem("x_loaded"); var_ready = sem("var_ready"); rstd_ready = sem("rstd_ready")
        xn_ready = sem("xn_ready"); xT_ready = sem("xT_ready"); xhi_ready = sem("xhi_ready")
        xlo_ready = sem("xlo_ready"); kproj = sem("kproj"); ksilu_ready = sem("ksilu_ready")
        gb_proj = sem("gb_proj"); g1_ready = sem("g1_ready")
        beta_ready = sem("beta_ready"); beta_out = sem("beta_out"); res_loaded = sem("res_loaded")
        qproj = sem("qproj"); q_ready = sem("q_ready"); vproj = sem("vproj"); v_ready = sem("v_ready")
        sq_ready = sem("sq_ready"); ss_ready = sem("ss_ready"); rk_ready = sem("rk_ready"); k_ready = sem("k_ready")
        gate_proj = sem("gate_proj"); gate_ready = sem("gate_ready")
        ktok = sem("ktok"); rhs_k_ready = sem("rhs_k_ready")
        kk_ready = sem("kk_ready"); tri_ready = sem("tri_ready"); m_ready = sem("m_ready")
        tri_out = sem("tri_out"); lane_in = sem("lane_in"); inv_ready = sem("inv_ready")
        inv_out = sem("inv_out"); inv_in = sem("inv_in")
        u0_mm = sem("u0_mm"); u0_ready = sem("u0_ready"); p_mm = sem("p_mm"); rhs2_ready = sem("rhs2_ready")
        u1_mm = sem("u1_mm"); uw_ready = sem("uw_ready")
        mw_mm = sem("mw_mm"); qeff_ready = sem("qeff_ready"); gh_mm = sem("gh_mm"); gh_ready = sem("gh_ready")
        chain_mm = sem("chain_mm"); state_ready = sem("state_ready")
        o_mm = sem("o_mm"); og_ready = sem("og_ready"); sq2_ready = sem("sq2_ready"); ms_ready = sem("ms_ready")
        ro_ready = sem("ro_ready"); ogn_ready = sem("ogn_ready"); ohi_ready = sem("ohi_ready"); olo_ready = sem("olo_ready")
        wo_mm = sem("wo_mm"); x2_ready = sem("x2_ready"); x2_stored = sem("x2_stored")
        dve_own = sem("dve_own"); ln_ready = sem("ln_ready"); ln2_ready = sem("ln2_ready"); pool_own = sem("pool_own")

        x_rows = x_in.rearrange("b (s t p) d -> b s p t d", p=P, t=TS)
        out_rows = out.rearrange("b (s t p) d -> b s p t d", p=P, t=TS)

        def at(b, s, per, k):
            return b * (SPB * per) + (s * per + k)

        CREDIT, STORE_CREDIT = 1, 16

        def over_spans(engine, begin, step, end):
            last = NBATCH - 1
            begin((0, 0), (0, 1))
            with engine.Fori(0, last) as b:
                step((b, 0), (b, 1), (b + 1, 0))
                step((b, 1), (b + 1, 0), (b + 1, 1))
            step((last, 0), (last, 1), None)
            end((last, 1))

        block = ctx.enter_context(nc.Block())

        @block.sync
        def _(sp):
            sp.sem_inc(x2_ready, CREDIT)
            sp.sem_inc(x2_stored, STORE_CREDIT)
            for n in range(NW):
                if n:
                    sp.wait_ge(w_split, 2 * n)
                sp.dma_start(stage[:, :], w_main[n]).then_inc(w_in, 16)
            sp.wait_ge(w_split, 2 * NW)
            sp.dma_start(stage[:, 0:KT * (HD + H)], w_gb).then_inc(w_in, 16)
            sp.dma_start(g2[:, :], w_g2).then_inc(c_in, 16)
            sp.dma_start(ident[:, :], ident_in).then_inc(c_in, 16)
            sp.dma_start(masks[:, :], masks_in).then_inc(c_in, 16)
            sp.dma_start(head_ones[:, :], ones_in).then_inc(c_in, 16)
            sp.dma_start(gnorm_half[:, :], g_norm).then_inc(c_in, 16)

            def to_lanes(b, s):
                sp.wait_ge(beta_ready, at(b, s, 1, 1))
                sp.dma_start(beta_dram.rearrange("u h i -> h u i"),
                             beta_t.rearrange("h (u i) -> h u i", i=NB)).then_inc(beta_out, 16)
                for t in range(TS):
                    sp.wait_ge(m_ready, at(b, s, TS, t + 1))
                    for pb in range(4):
                        i0 = NB * (pb % 2)
                        sp.dma_start(tri_dram[t * 4 + pb].rearrange("h j i -> j h i"),
                                     tri[NB * pb:NB * pb + NB, s, t, :, :, i0:i0 + NB].rearrange("j g e i -> j (g e) i")
                                     ).then_inc(tri_out, 16)
                sp.wait_ge(beta_out, at(b, s, 16, 16))
                sp.dma_start(lane_b[:, :], beta_dram.rearrange("u h i -> (u h) i")).then_inc(lane_in, 16)
                sp.wait_ge(tri_out, at(b, s, 16 * TS * 4, 16 * TS * 4))
                sp.dma_start(lane_t[:, :, :], tri_dram.rearrange("u h j i -> (u h) j i")).then_inc(lane_in, 16)

            def from_lanes(b, s):
                sp.wait_ge(inv_ready, at(b, s, 1, 1))
                sp.dma_start(inv_dram.rearrange("u h j i -> (u h) j i"), lane_t[:, :, :]).then_inc(inv_out, 16)
                sp.wait_ge(inv_out, at(b, s, 16, 16))
                for t in range(TS):
                    for pb in range(4):
                        sp.dma_start(inv_b[NB * pb:NB * pb + NB, t, :, :],
                                     inv_dram[t * 4 + pb].rearrange("h j i -> j h i")).then_inc(inv_in, 16)

            def load_residual(b, s):
                sp.wait_ge(x2_stored, at(b, s, 16, STORE_CREDIT))
                sp.dma_start(x_res[:, :, :], x_rows[b, s]).then_inc(res_loaded, 16)

            def store(b, s):
                sp.wait_ge(x2_ready, at(b, s, TS, CREDIT + TS))
                sp.dma_start(out_rows[b, s], x_res[:, :, :]).then_inc(x2_stored, 16)

            def begin(first, second):
                to_lanes(*first)
                from_lanes(*first)
                to_lanes(*second)

            def step(now, ahead, further):
                load_residual(*now)
                store(*now)
                from_lanes(*ahead)
                if further:
                    to_lanes(*further)

            def end(now):
                load_residual(*now)
                store(*now)

            over_spans(sp, begin, step, end)
            sp.wait_ge(x2_stored, STORE_CREDIT + NBATCH * SPB * 16)

        @block.gpsimd
        def _(pool):
            pool.memset(minus_half[:, :], -0.5).then_inc(pool_consts, 1)
            pool.memset(ln_eps[:, :], LN_EPS).then_inc(pool_consts, 1)
            pool.memset(state[:, 0, :], 0.0).then_inc(pool_consts, 1)
            pool.memset(eps_t[:, :], EPS).then_inc(pool_consts, 1)
            pool.wait_ge(pool_consts, 4)
            pool.wait_ge(c_in, 80)

            def inverse_std(b, s):
                pool.wait_ge(var_ready, at(b, s, TS, TS))
                pool.tensor_tensor(var_eps[:, :], mv[:, :, 1], ln_eps[:, :], ALU.add).then_inc(pool_own, 1)
                pool.wait_ge(pool_own, at(b, s, 1, 1))
                pool.tensor_tensor(rstd[:, :], var_eps[:, :], minus_half[:, :], ALU.pow).then_inc(rstd_ready, 1)

            def k_squares(b, s):
                for n in range(2):
                    pool.wait_ge(ksilu_ready, at(b, s, 2, n + 1))
                    v = kq[:, 2 * n:2 * n + 2, 0, :]
                    pool.tensor_tensor(sq[:, 2 * n:2 * n + 2, :], v, v, ALU.mult).then_inc(sq_ready, 1)

            def k_norm(b, s):
                for n in range(2):
                    pool.wait_ge(rk_ready, at(b, s, 2, n + 1))
                    g = slice(2 * n, 2 * n + 2)
                    pool.tensor_tensor(kq[:, g, 0, :], kq[:, g, 0, :], r_norm[:, g, :], ALU.mult).then_inc(k_ready, 1)

            def mask(b, s):
                m = masks[:, :].rearrange("p (o i) -> p o i", o=1).to_broadcast([P, H, 2 * C])
                for t in range(TS):
                    pool.wait_ge(tri_ready, at(b, s, TS * HPT, HPT * (t + 1)))
                    whole = tri[:, s, t, :, :, :].rearrange("p g e i -> p (g e) i")
                    pool.tensor_tensor(whole, whole, m, ALU.mult).then_inc(m_ready, 1)

            def output_squares(b, s):
                for t in range(TS):
                    pool.wait_ge(og_ready, at(b, s, 4, 2 * t + 2))
                    v = og[:, :, P * t:P * t + P]
                    pool.tensor_tensor(sq[:, :, P * t:P * t + P], v, v, ALU.mult).then_inc(sq2_ready, 1)

            def output_lo(b, s):
                pool.wait_ge(ohi_ready, at(b, s, 1, 1))
                pool.tensor_tensor(o_lo[:, :, :], og[:, :, :], o_hi[:, :, :].bitcast(F32), ALU.subtract).then_inc(olo_ready, 1)

            def begin(first, second):
                inverse_std(*first)
                inverse_std(*second)
                for span in (first, second):
                    k_squares(*span)
                    k_norm(*span)
                    mask(*span)

            def step(now, ahead, further):
                if further:
                    inverse_std(*further)
                output_squares(*now)
                output_lo(*now)
                if further:
                    k_squares(*further)
                    k_norm(*further)
                    mask(*further)

            def end(now):
                output_squares(*now)
                output_lo(*now)

            over_spans(pool, begin, step, end)

        @block.scalar
        def _(act):
            for n in range(NW):
                act.wait_ge(w_in, 16 * (n + 1))
                act.activation(w_hi[:, n, :, :].rearrange("p k n -> p (k n)"), stage[:, :], ACT.Copy).then_inc(w_split, 1)
            act.wait_ge(w_in, 16 * (NW + 1))
            act.activation(gb_hi[:, :, :].rearrange("p k n -> p (k n)"), stage[:, 0:KT * (HD + H)], ACT.Copy).then_inc(w_split, 1)
            act.wait_ge(pool_consts, 4)
            SILU_SET, LN_EXP_SET = "silu_and_others", "natural_log_exp_and_others"

            def load_x(b, s):
                act.dma_start(x_sp[:, :, :], x_rows[b, s]).then_inc(x_loaded, 16)

            def turned(b, s):
                for n in range(2):
                    act.wait_ge(xT_ready, at(b, s, 2, n + 1))
                    act.activation(x_hi[:, 2 * n:2 * n + 2, :], bank[3 * n][:, :], ACT.Copy).then_inc(xhi_ready, 1)

            def project_k(b, s, first=False):
                act.preload_act_table_set(SILU_SET)
                for n in range(2):
                    act.wait_ge(kproj, at(b, s, 2, n + 1))
                    act.activation(kq[:, 2 * n:2 * n + 2, 0, :], bank[1 + n][:, :].rearrange("p (g i) -> p g i", g=2), ACT.Silu).then_inc(ksilu_ready, 1)
                act.wait_ge(gb_proj, at(b, s, 1, 1))
                act.activation(g1, bank[0][0:HD, 0:SPAN], ACT.Copy).then_inc(g1_ready, 1)
                if not first:
                    act.wait_ge(beta_out, at(b, s, 16, 0))
                act.activation(beta_t, bank[0][HD:HD + H, 0:SPAN], ACT.Tanh, scale=0.5).then_inc(beta_ready, 1)

            def project_qv(b, s):
                for n in range(2):
                    act.wait_ge(qproj, at(b, s, 2, n + 1))
                    act.activation(kq[:, 2 * n:2 * n + 2, 1 + s, :], bank[3 - 2 * n][:, :].rearrange("p (g i) -> p g i", g=2),
                                   ACT.Silu).then_inc(q_ready, 1)
                for n in range(2):
                    act.wait_ge(gate_proj, at(b, s, 2, n + 1))
                    act.activation(gate[:, s, 2 * n:2 * n + 2, :], bank[2 - 2 * n][:, :], ACT.Tanh, scale=0.5).then_inc(gate_ready, 1)
                act.preload_act_table_set(LN_EXP_SET)
                for n in range(2):
                    v = r_norm[:, 2 * n:2 * n + 2, :]
                    act.wait_ge(ss_ready, at(b, s, 2, n + 1))
                    act.activation(v, bank[3 - 2 * n][:, :], ACT.Ln, bias=eps_t[:, 0:1]).then_inc(ln_ready, 1)
                for n in range(2):
                    v = r_norm[:, 2 * n:2 * n + 2, :]
                    act.wait_ge(ln_ready, at(b, s, 2, n + 1))
                    act.activation(v, v, ACT.Exp, scale=-0.5).then_inc(rk_ready, 1)
                for t in range(TS):
                    act.wait_ge(vproj, at(b, s, TS, t + 1))
                    act.activation(rhs[:, s, t, :, 0:HD], bank[2 - 2 * t][:, :].rearrange("p (h e) -> p h e", h=H),
                                   ACT.Copy).then_inc(v_ready, 1)
                for t in range(TS):
                    act.wait_ge(ktok, at(b, s, TS, t + 1))
                    act.activation(rhs[:, s, t, :, HD:2 * HD], bank[3 - 2 * t][:, :].rearrange("p (h e) -> p h e", h=H),
                                   ACT.Copy).then_inc(rhs_k_ready, 1)

            def triangles(b, s):
                for t in range(TS):
                    for e in range(HPT):
                        act.wait_ge(kk_ready, at(b, s, TS * HPT, t * HPT + e + 1))
                        act.activation(tri[:, s, t, :, e, :], bank[4 + e][:, :].rearrange("p (g i) -> p g i", g=KT),
                                       ACT.Copy).then_inc(tri_ready, 1)

            def solve(b, s):
                for t in range(TS):
                    act.wait_ge(u0_mm, at(b, s, TS, t + 1))
                    for n in range(2):
                        act.activation(uw[:, t, 8 * n:8 * n + 8, :], bank[4 + 2 * t + n][:, :].rearrange("p (h e) -> p h e", h=8),
                                       ACT.Copy).then_inc(u0_ready, 1)
                for t in range(TS):
                    act.wait_ge(u1_mm, at(b, s, TS, t + 1))
                    for n in range(2):
                        act.activation(uw[:, t, 8 * n:8 * n + 8, :], bank[4 + 2 * t + n][:, :].rearrange("p (h e) -> p h e", h=8),
                                       ACT.Copy).then_inc(uw_ready, 1)
                for half in range(2):
                    act.wait_ge(gh_mm, at(b, s, 2, half + 1))
                    act.activation(gh[:, half, :, :, :], bank[6 + half][:, :].rearrange("p (t g e) -> p t g e", t=TS, g=KT),
                                   ACT.Copy).then_inc(gh_ready, 1)

            def output(b, s):
                for n in range(2):
                    v = r_norm[:, 2 * n:2 * n + 2, :]
                    act.wait_ge(ms_ready, at(b, s, 2, n + 1))
                    act.activation(v, bank[4 + n][:, :], ACT.Ln, bias=eps_t[:, 0:1], scale=1.0 / (4 * HD)).then_inc(ln2_ready, 1)
                for n in range(2):
                    v = r_norm[:, 2 * n:2 * n + 2, :]
                    act.wait_ge(ln2_ready, at(b, s, 2, n + 1))
                    act.activation(v, v, ACT.Exp, scale=-0.5).then_inc(ro_ready, 1)
                act.wait_ge(ogn_ready, at(b, s, KT, KT))
                act.activation(o_hi[:, :, :], og[:, :, :], ACT.Copy).then_inc(ohi_ready, 1)

            def begin(first, second):
                load_x(*first)
                act.wait_ge(xn_ready, TS)
                load_x(*second)
                for span in (first, second):
                    turned(*span)
                    project_k(*span, first=span is first)
                    project_qv(*span)
                    triangles(*span)

            def step(now, ahead, further):
                if further:
                    act.wait_ge(xn_ready, at(*ahead, TS, TS))
                    load_x(*further)
                solve(*now)
                if further:
                    turned(*further)
                output(*now)
                if further:
                    project_k(*further)
                    project_qv(*further)
                    triangles(*further)

            def end(now):
                solve(*now)
                output(*now)

            over_spans(act, begin, step, end)

        @block.tensor
        def _(pe):
            pe.wait_ge(w_split, 2 * (NW + 1))
            pe.wait_ge(c_in, 80)
            pe.wait_ge(pool_consts, 4)
            pe.wait_ge(dve_consts, 1)
            awaited = pe.alloc_register("awaited")

            def after(value):
                pe.reg_mov(awaited, value)
                pe.wait_ge(pool_consts, 4)
                return awaited

            def features(out_ap, w, g):
                for k in range(KT):
                    last = split3(pe, out_ap, w_hi[:, w, k, P * g:P * g + P], w_lo[:, w, k, P * g:P * g + P],
                                  x_hi[:, k, :], x_lo[:, k, :], k == 0, k == KT - 1)
                return last

            def turned(b, s, first=False):
                pe.wait_ge(xn_ready, at(b, s, TS, TS))
                if not first:
                    pe.wait_ge(v_ready, at(b, s, TS, 0))
                    pe.wait_ge(rhs_k_ready, at(b, s, TS, 0))
                for n in range(2):
                    for g in range(2):
                        for t in range(TS):
                            k = 2 * n + g
                            last = pe.transpose(bank[3 * n][:, SPAN * g + P * t:SPAN * g + P * t + P],
                                                xn[:, t, P * k:P * k + P], ident[:, :])
                    last.then_inc(xT_ready, 1)

            def project_k(b, s):
                pe.wait_ge(xhi_ready, at(b, s, 2, 2))
                pe.wait_ge(xlo_ready, at(b, s, 2, 2))
                for n in range(2):
                    for g in range(2):
                        last = features(bank[1 + n][:, SPAN * g:SPAN * g + SPAN], 0, 2 * n + g)
                    last.then_inc(kproj, 1)
                for k in range(KT):
                    last = split3(pe, bank[0][0:HD + H, 0:SPAN], gb_hi[:, k, :], gb_lo[:, k, :],
                                  x_hi[:, k, :], x_lo[:, k, :], k == 0, k == KT - 1)
                last.then_inc(gb_proj, 1)

            def project_qv(b, s):
                for n in range(2):
                    if n:
                        pe.wait_ge(ksilu_ready, at(b, s, 2, 1))
                    for g in range(2):
                        last = features(bank[3 - 2 * n][:, SPAN * g:SPAN * g + SPAN], 1, 2 * n + g)
                    last.then_inc(qproj, 1)
                for n in range(2):
                    if n == 0:
                        pe.wait_ge(ksilu_ready, at(b, s, 2, 2))
                        pe.wait_ge(g1_ready, at(b, s, 1, 1))
                    else:
                        pe.wait_ge(beta_ready, at(b, s, 1, 1))
                    for g in range(2):
                        f = 2 * n + g
                        last = pe.matmul(bank[2 - 2 * n][:, SPAN * g:SPAN * g + SPAN], g2[:, P * f:P * f + P],
                                         g1, start=True, stop=True)
                    last.then_inc(gate_proj, 1)
                for n in range(2):
                    pe.wait_ge(sq_ready, at(b, s, 2, n + 1))
                    pe.wait_ge(q_ready, at(b, s, 2, n + 1))
                    pe.matmul(bank[3 - 2 * n][:, :], head_ones[:, :], sq[:, 2 * n:2 * n + 2, :],
                              start=True, stop=True).then_inc(ss_ready, 1)
                for t in range(TS):
                    pe.wait_ge(gate_ready, at(b, s, 2, t + 1))
                    for k in range(KT):
                        last = split3(pe, bank[2 - 2 * t][:, :], x_hi[:, k, P * t:P * t + P], x_lo[:, k, P * t:P * t + P],
                                      w_hi[:, 2, k, :], w_lo[:, 2, k, :], k == 0, k == KT - 1)
                    last.then_inc(vproj, 1)
                for t in range(TS):
                    pe.wait_ge(rk_ready, at(b, s, 2, 2))
                    pe.wait_ge(k_ready, at(b, s, 2, 2))
                    for g in range(KT):
                        last = pe.transpose(bank[3 - 2 * t][:, P * g:P * g + P], kq[:, g, 0, P * t:P * t + P], ident[:, :])
                    last.then_inc(ktok, 1)

            def triangles(b, s, before=None):
                if before:
                    pe.wait_ge(x2_ready, after(at(*before, TS, CREDIT + TS)))
                elif s:
                    pe.wait_ge(tri_ready, TS * HPT)
                for t in range(TS):
                    for e in range(HPT):
                        if t:
                            pe.wait_ge(tri_ready, after(at(b, s, TS * HPT, e + 1)))
                        rows = slice(HD * e, HD * e + HD)
                        for g in range(KT):
                            for half in range(2):
                                i0 = P * t + C * half
                                last = pe.matmul(bank[4 + e][C * half:C * half + C, 2 * C * g:2 * C * g + 2 * C],
                                                 kq[rows, g, 0, i0:i0 + C], kq[rows, g, 0:s + 2:s + 1, i0:i0 + C],
                                                 start=True, stop=True)
                        last.then_inc(kk_ready, 1)

            def solve(b, s, ahead):
                pe.wait_ge(m_ready, at(b, s, TS, TS))
                pe.wait_ge(inv_in, at(b, s, 16 * TS * 4, 16 * TS * 4))
                pe.wait_ge(rhs_k_ready, at(b, s, TS, TS))
                pe.wait_ge(v_ready, at(b, s, TS, TS))
                if ahead:
                    pe.wait_ge(tri_ready, after(at(*ahead, TS * HPT, TS * HPT)))
                else:
                    pe.wait_ge(x2_ready, after(at(b, s, TS, CREDIT)))

                def blocks(t, lower, weights, moving):
                    for h in range(H):
                        for half in range(2):
                            src = NB * (2 * half + (1 if lower == 2 else 0))
                            dst = NB * (2 * half + (1 if lower else 0))
                            last = pe.matmul(bank[4 + 2 * t + h // 8][dst:dst + NB, 2 * HD * (h % 8):2 * HD * (h % 8) + 2 * HD],
                                             weights(h, src), moving(src, h), start=True, stop=True)
                    return last

                for t in range(TS):
                    blocks(t, 0, lambda h, r: inv_b[r:r + NB, t, h, :], lambda r, h: rhs[r:r + NB, s, t, h, :]).then_inc(u0_mm, 1)
                for t in range(TS):
                    pe.wait_ge(u0_ready, after(at(b, s, 2 * TS, 2 * t + 2)))
                    blocks(t, 1, lambda h, r: tri[r:r + NB, s, t, h // HPT, h % HPT, NB:2 * NB], lambda r, h: uw[r:r + NB, t, h, :]).then_inc(p_mm, 1)
                for t in range(TS):
                    pe.wait_ge(rhs2_ready, after(at(b, s, 2 * TS, 2 * t + 2)))
                    blocks(t, 2, lambda h, r: inv_b[r:r + NB, t, h, :], lambda r, h: rhs2[r:r + NB, t, h, :]).then_inc(u1_mm, 1)

                pe.wait_ge(uw_ready, after(at(b, s, 2 * TS, 2 * TS)))
                for half in range(2):
                    rows = slice(C * half, C * half + C)
                    for t in range(TS):
                        for h in range(H):
                            g, e = h // HPT, h % HPT
                            last = pe.matmul(bank[4 + half][HD * e:HD * e + HD, (t * KT + g) * C:(t * KT + g) * C + C],
                                             uw[rows, t, h, HD:2 * HD], tri[rows, s, t, g, e, C:2 * C], start=True, stop=True)
                    last.then_inc(mw_mm, 1)
                for half in range(2):
                    rows = slice(C * half, C * half + C)
                    for t in range(TS):
                        for h in range(H):
                            g, e = h // HPT, h % HPT
                            c0 = (t * KT + g) * 2 * HD
                            o = bank[6 + half][HD * e:HD * e + HD, :]
                            pe.matmul(o[:, c0:c0 + HD], uw[rows, t, h, HD:2 * HD], rhs[rows, s, t, h, HD:2 * HD],
                                      start=True, stop=True)
                            last = pe.matmul(o[:, c0 + HD:c0 + 2 * HD], rhs[rows, s, t, h, HD:2 * HD], uw[rows, t, h, 0:HD],
                                             start=True, stop=True)
                    last.then_inc(gh_mm, 1)

                for c in range(2 * TS):
                    t, half = c // 2, c % 2
                    if c == 0:
                        done = after(at(b, s, 2, 2))
                        pe.wait_ge(gh_ready, done)
                        pe.wait_ge(qeff_ready, done)
                    else:
                        pe.wait_ge(state_ready, after(at(b, s, 4, c)))
                    for h in range(H):
                        g, e = h // HPT, h % HPT
                        r = slice(HD * e, HD * e + HD)
                        last = pe.matmul(bank[4][r, P * c + HD * g:P * c + HD * g + HD], gh[r, half, t, g, 0:HD],
                                         state[r, 4 * s + c, HD * g:HD * g + HD], start=True, stop=True)
                    last.then_inc(chain_mm, 1)
                    rows = slice(C * half, C * half + C)
                    o = [bank[6 + half][HD * (h % HPT):HD * (h % HPT) + HD,
                                        C * (KT * t + h // HPT):C * (KT * t + h // HPT) + C] for h in range(H)]
                    for h in range(H):
                        g, e = h // HPT, h % HPT
                        pe.matmul(o[h], uw[rows, t, h, 0:HD], tri[rows, s, t, g, e, C:2 * C],
                                  start=g == 0, stop=False, skip_group_check=True)
                    for h in range(H):
                        g, e = h // HPT, h % HPT
                        r = slice(HD * e, HD * e + HD)
                        last = pe.matmul(o[h], state[r, 4 * s + c, HD * g:HD * g + HD],
                                         kq[r, g, 1 + s, P * t + C * half:P * t + C * half + C],
                                         start=False, stop=g == KT - 1, skip_group_check=True)
                    last.then_inc(o_mm, 1)

            def output_sums(b, s):
                pe.wait_ge(sq2_ready, at(b, s, TS, TS))
                pe.wait_ge(state_ready, at(b, s, 4, 4))
                for n in range(2):
                    pe.matmul(bank[4 + n][:, :], head_ones[:, :], sq[:, 2 * n:2 * n + 2, :],
                              start=True, stop=True).then_inc(ms_ready, 1)

            def output(b, s):
                pe.wait_ge(ohi_ready, at(b, s, 1, 1))
                pe.wait_ge(olo_ready, at(b, s, 1, 1))
                for t in range(TS):
                    for k in range(KT):
                        last = split3(pe, bank[6 + t][:, :], o_hi[:, k, P * t:P * t + P], o_lo[:, k, P * t:P * t + P],
                                      w_hi[:, 3, k, :], w_lo[:, 3, k, :], k == 0, k == KT - 1)
                    last.then_inc(wo_mm, 1)

            def begin(first, second):
                for span in (first, second):
                    turned(*span, first=span is first)
                    project_k(*span)
                    project_qv(*span)
                    triangles(*span)

            def step(now, ahead, further):
                solve(*now, ahead)
                if further:
                    turned(*further)
                output_sums(*now)
                if further:
                    project_k(*further)
                output(*now)
                if further:
                    project_qv(*further)
                    triangles(*further, now)

            def end(now):
                solve(*now, None)
                output_sums(*now)
                output(*now)

            over_spans(pe, begin, step, end)

        @block.vector
        def _(dve):
            for n in range(NW):
                dve.wait_ge(w_split, 2 * n + 1)
                dve.tensor_tensor(w_lo[:, n, :, :].rearrange("p k n -> p (k n)"), stage[:, :],
                                  w_hi[:, n, :, :].rearrange("p k n -> p (k n)").bitcast(F32), ALU.subtract).then_inc(w_split, 1)
            dve.wait_ge(w_split, 2 * NW + 1)
            dve.tensor_tensor(gb_lo[:, :, :].rearrange("p k n -> p (k n)"), stage[:, 0:KT * (HD + H)],
                              gb_hi[:, :, :].rearrange("p k n -> p (k n)").bitcast(F32), ALU.subtract).then_inc(w_split, 1)
            dve.wait_ge(c_in, 80)
            dve.tensor_scalar(gnorm_half[:, :], gnorm_half[:, :], 0.5, None, ALU.mult).then_inc(dve_consts, 1)
            dve.wait_ge(dve_consts, 1)
            dve.wait_ge(pool_consts, 4)
            own = [0]

            def mark(ins):
                own[0] += 1
                ins.then_inc(dve_own, 1)

            def clear_marks():
                dve.wait_ge(dve_own, own[0])
                dve.sem_clear(dve_own)
                own[0] = 0

            def statistics(b, s):
                dve.wait_ge(x_loaded, at(b, s, 16, 16))
                for t in range(TS):
                    mark(dve.bn_stats(stats[:, t, :], x_sp[:, t, :]))
                for t in range(TS):
                    dve.wait_ge(dve_own, own[0] - TS + 1 + t)
                    dve.bn_aggr(mv[:, t, :], stats[:, t, :]).then_inc(var_ready, 1)

            def normalise(b, s, first=False):
                if not first:
                    dve.wait_ge(k_ready, at(b, s, 2, 0))
                dve.wait_ge(var_ready, at(b, s, TS, TS))
                dve.wait_ge(rstd_ready, at(b, s, 1, 1))
                for t in range(TS):
                    dve.tensor_scalar(xn[:, t, :], x_sp[:, t, :], mv[:, t, 0:1], rstd[:, t:t + 1],
                                      ALU.subtract, ALU.mult).then_inc(xn_ready, 1)

            def split_x(b, s):
                for n in range(2):
                    dve.wait_ge(xhi_ready, at(b, s, 2, n + 1))
                    dve.tensor_tensor(x_lo[:, 2 * n:2 * n + 2, :], bank[3 * n][:, :].rearrange("p (g i) -> p g i", g=2),
                                      x_hi[:, 2 * n:2 * n + 2, :].bitcast(F32), ALU.subtract).then_inc(xlo_ready, 1)

            def invert(b, s, columns):
                if columns[0] == 1:
                    dve.wait_ge(lane_in, at(b, s, 32, 32))
                    mark(dve.tensor_scalar(lane_b[:, :], lane_b[:, :], 1.0, None, ALU.add))
                    dve.wait_ge(dve_own, own[0])
                    mark(dve.scalar_tensor_tensor(lane_t[:, :, :], lane_t[:, :, :], -1.0,
                                                  lane_b[:, :].rearrange("p (o i) -> p o i", o=1).to_broadcast([P, NB, NB]),
                                                  ALU.mult, ALU.mult))
                for m in columns:
                    n = NB - 1 - m
                    prod = lane_p[:, 0:m * n].rearrange("p (j i) -> p j i", j=m)
                    dve.wait_ge(dve_own, own[0])
                    mark(dve.tensor_tensor(prod, lane_t[:, 0:m, m:m + 1].to_broadcast([P, m, n]),
                                           lane_t[:, m:m + 1, m + 1:NB].to_broadcast([P, m, n]), ALU.mult))
                    dve.wait_ge(dve_own, own[0])
                    mark(dve.tensor_tensor(lane_t[:, 0:m, m + 1:NB], lane_t[:, 0:m, m + 1:NB], prod, ALU.add))
                if columns[-1] == NB - 2:
                    dve.wait_ge(dve_own, own[0])
                    mark(dve.tensor_tensor(lane_t[:, :, :], lane_t[:, :, :],
                                           lane_b[:, :].rearrange("p (j o) -> p j o", o=1).to_broadcast([P, NB, NB]), ALU.mult))
                    dve.wait_ge(dve_own, own[0])
                    dve.tensor_copy(lane_t[:, :, :].rearrange("p j i -> p (j i)")[:, 0:NB * NB:NB + 1],
                                    lane_b[:, :]).then_inc(inv_ready, 1)

            def solve(b, s):
                for t in range(TS):
                    dve.wait_ge(p_mm, at(b, s, TS, t + 1))
                    for n in range(2):
                        hs = slice(8 * n, 8 * n + 8)
                        dve.tensor_tensor(rhs2[:, t, hs, :], rhs[:, s, t, hs, :],
                                          bank[4 + 2 * t + n][:, :].rearrange("p (h e) -> p h e", h=8),
                                          ALU.subtract).then_inc(rhs2_ready, 1)
                for half in range(2):
                    dve.wait_ge(mw_mm, at(b, s, 2, half + 1))
                    qv = kq[:, :, 1 + s, :].rearrange("p g (t f i) -> p t g f i", t=TS, f=2)[:, :, :, half, :]
                    pv = bank[4 + half][:, :].rearrange("p (t g i) -> p t g i", t=TS, g=KT)
                    for t in range(TS):
                        last = dve.tensor_tensor(qv[:, t], qv[:, t], pv[:, t], ALU.subtract)
                    last.then_inc(qeff_ready, 1)
                for c in range(2 * TS):
                    t, half = c // 2, c % 2
                    if c == 0:
                        dve.wait_ge(gh_ready, at(b, s, 2, 2))
                    if s or c:
                        dve.wait_ge(state_ready, at(b, s, 4, c))
                    mark(dve.tensor_tensor(state[:, 4 * s + c + 1, :].rearrange("p (g e) -> p g e", g=KT),
                                           state[:, 4 * s + c, :].rearrange("p (g e) -> p g e", g=KT),
                                           gh[:, half, t, :, HD:2 * HD], ALU.add))
                    dve.wait_ge(dve_own, own[0])
                    dve.wait_ge(chain_mm, at(b, s, 4, c + 1))
                    dve.tensor_tensor(state[:, 4 * s + c + 1, :], state[:, 4 * s + c + 1, :], bank[4][:, P * c:P * c + P],
                                      ALU.subtract).then_inc(state_ready, 1)
                    if c == 0:
                        dve.wait_ge(gate_ready, at(b, s, 2, 2))
                    dve.wait_ge(o_mm, at(b, s, 4, c + 1))
                    i0 = P * t + C * half
                    dve.scalar_tensor_tensor(og[:, :, i0:i0 + C], gate[:, s, :, i0:i0 + C], 1.0,
                                             bank[6 + half][:, C * KT * t:C * KT * t + C * KT].rearrange("p (g i) -> p g i", g=KT),
                                             ALU.add, ALU.mult).then_inc(og_ready, 1)

            def output(b, s):
                dve.wait_ge(sq2_ready, at(b, s, TS, TS))
                for g in range(KT):
                    dve.wait_ge(ro_ready, at(b, s, 2, g // 2 + 1))
                    dve.scalar_tensor_tensor(og[:, g, :], og[:, g, :], gnorm_half[:, g:g + 1], r_norm[:, g, :],
                                             ALU.mult, ALU.mult).then_inc(ogn_ready, 1)

            def add_residual(b, s):
                dve.wait_ge(res_loaded, at(b, s, 16, 16))
                for t in range(TS):
                    dve.wait_ge(wo_mm, at(b, s, TS, t + 1))
                    dve.tensor_tensor(x_res[:, t, :], x_res[:, t, :], bank[6 + t][:, :], ALU.add).then_inc(x2_ready, 1)

            FIRST_COLUMNS, LAST_COLUMNS = range(1, NB // 2), range(NB // 2, NB - 1)

            def begin(first, second):
                for span in (first, second):
                    statistics(*span)
                    normalise(*span, first=span is first)
                    split_x(*span)
                invert(*first, range(1, NB - 1))
                clear_marks()

            def step(now, ahead, further):
                if further:
                    statistics(*further)
                    normalise(*further)
                solve(*now)
                if further:
                    split_x(*further)
                output(*now)
                invert(*ahead, FIRST_COLUMNS)
                add_residual(*now)
                invert(*ahead, LAST_COLUMNS)
                clear_marks()

            def end(now):
                solve(*now)
                output(*now)
                add_residual(*now)
                clear_marks()

            over_spans(dve, begin, step, end)


NQ = 4
NKV = 8
DH = D // (NQ * NKV)
DKV = NKV * DH
NE, RANK = 8, 16
ER = NE * RANK
QUADS = NQ * NKV // 4
SR = 3 * DH + 1
LW = D // 2 + ER // 2 + NE
RW = D // 2 + ER // 2
NH = NQ * NKV
SCORE_LAG = 7
AV_LAG = SCORE_LAG + 1
AV_SLOTS = ((0, 1), (1, 1), (2, 0), (2, 1))
TURN_LAG = AV_LAG + 3
OUT_LAG = TURN_LAG + 1
PROBS = 7


def token_layers(nc, dims, x2_in, w_ffn, b_ffn, lora_b, gate_b, w_q, w_kv, mem_aug_in, mem_w_in, ident_in, rank_mask_in, sel_in, head_rows_in, out):
    NBATCH, SEQ = dims
    NT = SEQ // P
    with ExitStack() as ctx:
        def sb(name, shape, dt=F32):
            return ctx.enter_context(nc.sbuf_tensor(name, shape, dt))

        def sem(name):
            return ctx.enter_context(nc.semaphore(name))

        ps = ctx.enter_context(nc.psum_tensor("row_psum", [P, 8, 512], F32))

        FW = LW + RW
        wf_hi = sb("wf_hi", [P, KT, FW], F32R)
        wf_lo = sb("wf_lo", [P, KT, FW], F32R)
        lb_hi = sb("lb_hi", [P, D], F32R)
        lb_lo = sb("lb_lo", [P, D], F32R)
        wq_hi = sb("wq_hi", [P, KT, D], F32R)
        wq_lo = sb("wq_lo", [P, KT, D], F32R)
        wkv_hi = sb("wkv_hi", [P, KT, 2 * DKV], F32R)
        wkv_lo = sb("wkv_lo", [P, KT, 2 * DKV], F32R)
        mem_aug = sb("mem_aug", [P, DKV + 1])
        mem_w = sb("mem_w", [P, 1])
        mem_wc = sb("mem_wc", [P, 1])
        bias_bc = sb("bias_bc", [P, D])
        gate_b_bc = sb("gate_b_bc", [P, NE])
        rank_mask = sb("rank_mask", [P, NE, NE])
        ident2 = sb("ident2", [P, P])
        minus_half = sb("minus_half4", [P, NT])
        ln_eps = sb("ln_eps4", [P, NT])

        sel = sb("sel", [P, 4, P], F32R)
        head_rows = sb("head_rows", [P, 2, 2])

        xs = sb("xs", [P, 2, NT, D])
        stats = sb("stats4", [P, NT, 6])
        mv = sb("mv4", [P, NT, 2])
        var_eps = sb("var_eps4", [P, NT])
        rstd = sb("rstd4", [P, NT])
        x_hi = sb("xr_hi", [P, KT, SEQ], F32R)
        x_lo = sb("xr_lo", [P, KT, SEQ], F32R)
        lg = sb("lg", [P, NT, NE])
        lmax = sb("lmax", [P, NT])
        lp = sb("lp", [P, NT, NE])
        rank = sb("rank", [P, NT * NE])
        psum_g = sb("psum_g", [P, NT])
        xat_hi = sb("xat_hi", [P, SEQ], F32R)
        xat_lo = sb("xat_lo", [P, SEQ], F32R)
        q_stack = sb("q_stack", [P, NQ * NKV // 2, SEQ], F32R)
        k_stack = sb("k_stack", [P, NKV, SEQ], F32R)
        v_aug = sb("v_aug", [P, NT, NKV, 32])
        smax = sb("smax", [P, NQ * NKV, NT])
        shift = sb("shift", [4, SEQ], F32R)
        mem_rc = sb("mem_rc", [P, NT, NQ])
        av_sb = sb("av_sb", [P, 2, SEQ])
        av_rc = sb("av_rc", [P, NT, 4])
        av_n = sb("av_n", [P, 2, NT, 4, DH])
        probs = sb("probs", [P, PROBS, NT, SEQ])
        pool_mem = probs[:, :, :, :].rearrange("p h t s -> p (h t s)")

        def part(n, size):
            return pool_mem[:, n:n + size]
        xn = part(0, NT * D).rearrange("p (t d) -> p t d", t=NT)
        q_hi, q_lo, k_hi, k_lo = x_hi, x_lo, xat_hi, xat_lo
        q_elu = part(2048, NQ * SEQ).rearrange("p (n s) -> p n s", n=NQ)
        q_exp = part(4096, NQ * SEQ).rearrange("p (n s) -> p n s", n=NQ)
        vT = part(6144, SEQ)
        a_mem = part(6656, NT * D).rearrange("p (t d) -> p t d", t=NT)
        cmp_gt = part(8704, NT * NE * NE).rearrange("p (t e j) -> p t e j", t=NT, e=NE)
        cmp_eq = part(8960, NT * NE * NE).rearrange("p (t e j) -> p t e j", t=NT, e=NE)
        xa = part(9216, NT * ER).rearrange("p (t r) -> p t r", t=NT)
        stage = part(0, KT * FW)

        w_in = sem("row_w_in"); w_hi_done = sem("row_w_hi"); w_lo_done = sem("row_w_lo"); c_in = sem("row_c_in")
        pool_consts = sem("row_pool_consts"); mem_tanh = sem("mem_tanh"); dve_consts = sem("row_dve_consts")
        x_loaded = [sem("row_x_loaded0"), sem("row_x_loaded1")]
        x_stored = sem("row_x_stored")
        var_ready = sem("row_var"); var_eps_ready = sem("row_var_eps"); rstd_ready = sem("row_rstd"); xn_ready = sem("row_xn"); bias_added = sem("bias_added")
        xT_ready = sem("row_xT"); xhi_ready = sem("row_xhi"); xlo_ready = sem("row_xlo")
        left_mm = sem("left_mm"); right_mm = sem("right_mm"); xa_ready = sem("xa_ready"); base_added = sem("base_added"); ldiff_ready = sem("ldiff_ready")
        lp_ready = sem("lp_ready"); xaw_ready = sem("xaw_ready"); xaT_mm = sem("xaT_mm"); xathi_ready = sem("xathi_ready")
        xatlo_ready = sem("xatlo_ready"); lora_mm = sem("lora_mm"); ffn_added = sem("ffn_added")
        q_mm = sem("q_mm"); qhi_ready = sem("row_qhi"); qexp_ready = sem("qexp_ready"); qlo_ready = sem("row_qlo"); qelu_ready = sem("qelu_ready")
        k_mm = sem("row_k_mm"); khi_ready = sem("row_khi"); klo_ready = sem("row_klo"); v_mm = sem("row_v_mm"); vT_ready = sem("vT_ready")
        vtok_mm = sem("vtok_mm"); v_ready = sem("row_v_ready")
        ksel_mm = sem("ksel_mm"); kstack_ready = sem("kstack_ready"); qsel_mm = sem("qsel_mm"); qstack_ready = sem("qstack_ready")
        mem_mm = sem("mem_mm"); amem_ready = sem("amem_ready"); amem_added = sem("amem_added")
        max_mm = sem("max_mm"); max_ready = sem("max_ready"); maxT_mm = sem("maxT_mm"); shift_ready = sem("shift_ready"); shift_in = sem("shift_in")
        score_mm = sem("score_mm"); exp_ready = sem("exp_ready"); av_mm = sem("av_mm"); av_ready = sem("av_ready")
        avT_mm = sem("avT_mm"); avn_ready = sem("avn_ready"); adot_added = sem("adot_added"); dve_own = sem("row_dve_own")

        x2_rows = x2_in.rearrange("b (t p) d -> b p t d", p=P)
        out_rows = out.rearrange("b (t p) d -> b p t d", p=P)
        STORE_CREDIT, FFN_CREDIT = 16, 1

        def at(b, per, k):
            return b * per + k

        def head(quad, i):
            return divmod(4 * quad + i, NKV)

        HP = NKV // 2

        def turned_before(quad):
            return sum(4 * q + 3 + TURN_LAG < 4 * quad + 4 for q in range(QUADS))

        def maxima_before(quad):
            return sum(4 * q + 4 <= 4 * quad + 3 + TURN_LAG for q in range(QUADS))

        block = ctx.enter_context(nc.Block())

        @block.sync
        def _(sp):
            sp.sem_inc(x_stored, STORE_CREDIT)
            for n, (src, size) in enumerate(((w_ffn, KT * FW), (lora_b, D), (w_q, KT * D), (w_kv, KT * 2 * DKV), (sel_in, 4 * P))):
                if n:
                    sp.wait_ge(w_lo_done, n)
                sp.dma_start(stage[:, 0:size], src).then_inc(w_in, 16)
            for dst, src in ((mem_aug, mem_aug_in), (mem_w, mem_w_in), (bias_bc, b_ffn), (gate_b_bc, gate_b),
                             (ident2, ident_in)):
                sp.dma_start(dst[:, :], src).then_inc(c_in, 16)
            sp.dma_start(head_rows[:, :, :].rearrange("p h c -> p (h c)"), head_rows_in).then_inc(c_in, 16)
            sp.dma_start(rank_mask[:, :, :].rearrange("p e j -> p (e j)"), rank_mask_in).then_inc(c_in, 16)
            sp.dma_start(xs[:, 0, :, :], x2_rows[0]).then_inc(x_loaded[0], 16)
            with sp.Fori(0, NBATCH // 2) as bb:
                for par in range(2):
                    b = bb * 2 + par
                    sp.wait_ge(x_stored, at(b, 16, STORE_CREDIT))
                    ahead = bb * 2 + 1 if par == 0 else (bb * 2 + 2) % NBATCH
                    sp.dma_start(xs[:, 1 - par, :, :], x2_rows[ahead]).then_inc(x_loaded[1 - par], 16)
                    for quad in range(QUADS):
                        sp.wait_ge(shift_ready, at(b, QUADS, quad + 1))
                        for i in range(4):
                            n, h = head(quad, i)
                            r0 = 64 * (h % 2) + 3 * DH
                            sp.dma_start(q_stack[r0:r0 + 1, n * HP + h // 2, :].bitcast(F32),
                                         shift[i:i + 1, :].bitcast(F32)).then_inc(shift_in, 16)
                    sp.wait_ge(ffn_added, at(b, 2 * NT, FFN_CREDIT + 2 * NT))
                    sp.dma_start(out_rows[b], xs[:, par, :, :]).then_inc(x_stored, 16)
            sp.wait_ge(x_stored, STORE_CREDIT + NBATCH * 16)
            sp.wait_ge(x_loaded[0], 16 * (NBATCH // 2 + 1))

        @block.gpsimd
        def _(pool):
            pool.memset(minus_half[:, :], -0.5).then_inc(pool_consts, 1)
            pool.memset(ln_eps[:, :], LN_EPS).then_inc(pool_consts, 1)
            pool.memset(v_aug[:, :, :, :], 1.0).then_inc(pool_consts, 1)
            pool.wait_ge(pool_consts, 3)
            pool.wait_ge(c_in, 112)

            def inverse_std(b, f):
                pool.wait_ge(var_ready, at(b, 3 * NT, NT * (f + 1)))
                pool.tensor_tensor(var_eps[:, :], mv[:, :, 1], ln_eps[:, :], ALU.add).then_inc(var_eps_ready, 1)
                pool.wait_ge(var_eps_ready, at(b, 3, f + 1))
                pool.tensor_tensor(rstd[:, :], var_eps[:, :], minus_half[:, :], ALU.pow).then_inc(rstd_ready, 1)

            inverse_std(0, 0)
            with pool.Fori(0, NBATCH // 2) as bb:
                for par in range(2):
                    b = bb * 2 + par

                    def add_bias(f):
                        pool.wait_ge(xn_ready, at(b, 3 * NT, NT * (2 * f + 1)))
                        for t in range(NT):
                            pool.tensor_tensor(xs[:, par, t, :], xs[:, par, t, :], bias_bc[:, :], ALU.add).then_inc(bias_added, 1)

                    add_bias(0)
                    inverse_std(b, 1)
                    for t in range(NT):
                        pool.wait_ge(amem_ready, at(b, NT, t + 1))
                        pool.tensor_tensor(xs[:, par, t, :], xs[:, par, t, :], a_mem[:, t, :], ALU.add).then_inc(amem_added, 1)
                    for quad in range(QUADS):
                        if quad == 0:
                            pool.wait_ge(amem_added, at(b, NT, NT))
                        pool.wait_ge(avn_ready, at(b, QUADS, quad + 1))
                        xq = xs[:, par, :, 64 * quad:64 * quad + 64]
                        pool.tensor_tensor(xq, xq, av_n[:, quad % 2, :, :, :].rearrange("p t h e -> p t (h e)"), ALU.add).then_inc(adot_added, 1)
                    inverse_std(b, 2)
                    add_bias(1)
                    inverse_std(b, 3)

        @block.scalar
        def _(act):
            for n, (dst, size) in enumerate(((wf_hi, KT * FW), (lb_hi, D), (wq_hi, KT * D), (wkv_hi, KT * 2 * DKV), (sel, 4 * P))):
                act.wait_ge(w_in, 16 * (n + 1))
                d2 = dst[:, :] if n == 1 else dst[:, :, :].rearrange("p k n -> p (k n)")
                act.activation(d2, stage[:, 0:size], ACT.Copy).then_inc(w_hi_done, 1)
            act.wait_ge(c_in, 112)
            act.activation(mem_w[:, :], mem_w[:, :], ACT.Tanh, scale=0.5).then_inc(mem_tanh, 1)

            def norm_hi(b, f):
                for t in range(NT):
                    act.wait_ge(xT_ready, at(b, 3 * NT, NT * f + t + 1))
                    act.activation(x_hi[:, :, P * t:P * t + P], ps[:, t, :].rearrange("p (k i) -> p k i", k=KT), ACT.Copy).then_inc(xhi_ready, 1)

            norm_hi(0, 0)
            with act.Fori(0, NBATCH // 2) as bb:
                for par in range(2):
                    b = bb * 2 + par

                    def ffn(f):
                        for c, done in ((1, left_mm), (0, right_mm)):
                            for t in range(NT):
                                act.wait_ge(done, at(b, 2 * NT, NT * f + t + 1))
                                act.activation(xa[:, t, ER // 2 * (1 - c):ER // 2 * (2 - c)],
                                               ps[:, 4 * c + t, D // 2:D // 2 + ER // 2], ACT.Copy).then_inc(xa_ready, 1)
                            if c == 1:
                                act.wait_ge(ldiff_ready, at(b, 2, f + 1))
                                act.activation(lp[:, :, :], lp[:, :, :], ACT.Exp).then_inc(lp_ready, 1)
                        act.wait_ge(xaT_mm, at(b, 2, f + 1))
                        act.activation(xat_hi[:, :], ps[:, 0, :], ACT.Copy).then_inc(xathi_ready, 1)

                    ffn(0)
                    norm_hi(b, 1)
                    act.wait_ge(v_mm, at(b, 1, 1))
                    act.activation(k_hi[:, :], ps[:, 0, :], ACT.Copy).then_inc(khi_ready, 1)
                    act.activation(vT, ps[:, 1, :], ACT.Copy).then_inc(vT_ready, 1)
                    for n in range(NQ):
                        act.activation(q_hi[:, n, :], ps[:, 4 + n, :], ACT.Copy).then_inc(qhi_ready, 1)
                        act.activation(q_exp[:, n, :], ps[:, 4 + n, :], ACT.Exp).then_inc(qexp_ready, 1)
                    for m in range(NQ * HP):
                        act.wait_ge(qsel_mm, at(b, NQ * HP, m + 1))
                        act.activation(q_stack[:, m, :], ps[:, m % 4, :], ACT.Copy).then_inc(qstack_ready, 1)
                    act.wait_ge(amem_added, at(b, NT, NT))
                    act.wait_ge(vtok_mm, at(b, 1, 1))
                    for g in range(NH + OUT_LAG):
                        h = g - SCORE_LAG
                        for j in range(2):
                            if 0 <= h < NH:
                                act.wait_ge(score_mm, at(b, 2 * NH, 2 * h + j + 1))
                                if h >= PROBS and j == 0:
                                    act.wait_ge(av_mm, at(b, QUADS, (h - PROBS) // 4 + 1))
                                act.activation(probs[:, h % PROBS, 2 * j:2 * j + 2, :], ps[:, 2 * j:2 * j + 2, :], ACT.Exp,
                                               scale=float(DH) ** -0.5).then_inc(exp_ready, 1)
                        quad, i = divmod(g - 3, 4)
                        if i == 1 and 0 <= quad < QUADS:
                            act.wait_ge(maxT_mm, at(b, QUADS, quad + 1))
                            if quad:
                                act.wait_ge(shift_in, at(b, 64 * QUADS, 64 * quad))
                            act.activation(shift[:, :], ps[0:4, 7, :], ACT.Copy, scale=-1.0).then_inc(shift_ready, 1)
                        quad, i = divmod(g - 3 - AV_LAG, 4)
                        if i == 2 and 0 <= quad < QUADS:
                            act.wait_ge(av_mm, at(b, QUADS, quad + 1))
                            if quad >= 2:
                                act.wait_ge(avT_mm, at(b, QUADS, quad - 1))
                            act.activation(av_sb[:, quad % 2, :], ps[:, 6, :], ACT.Copy).then_inc(av_ready, 1)
                    norm_hi(b, 2)
                    ffn(1)
                    norm_hi(b, 3)

        @block.tensor
        def _(pe):
            pe.wait_ge(w_lo_done, 4)
            pe.wait_ge(w_hi_done, 5)
            pe.wait_ge(c_in, 112)
            pe.wait_ge(pool_consts, 3)

            def turned(b, f):
                for t in range(NT):
                    pe.wait_ge(xn_ready, at(b, 3 * NT, NT * f + t + 1))
                    for k in range(KT):
                        last = pe.transpose(ps[:, t, P * k:P * k + P], xn[:, t, P * k:P * k + P], ident2[:, :])
                    last.then_inc(xT_ready, 1)

            awaited = pe.alloc_register("row_awaited")

            def after(value):
                pe.reg_mov(awaited, value)
                pe.wait_ge(pool_consts, 3)
                return awaited

            turned(0, 0)
            with pe.Fori(0, NBATCH // 2) as bb:
                for par in range(2):
                    b = bb * 2 + par

                    def ffn(f):
                        for t in range(NT):
                            pe.wait_ge(xhi_ready, at(b, 3 * NT, NT * (2 * f) + t + 1))
                            pe.wait_ge(xlo_ready, at(b, 3 * NT, NT * (2 * f) + t + 1))
                            if f:
                                if t == 0:
                                    pe.wait_ge(avn_ready, at(b, QUADS, QUADS))
                            else:
                                pe.wait_ge(ffn_added, at(b, 2 * NT, FFN_CREDIT))
                            tok = slice(P * t, P * t + P)
                            for k in range(KT):
                                last = split3(pe, ps[:, 4 + t, 0:LW], x_hi[:, k, tok], x_lo[:, k, tok],
                                              wf_hi[:, k, 0:LW], wf_lo[:, k, 0:LW], k == 0, k == KT - 1)
                            last.then_inc(left_mm, 1)
                        for t in range(NT):
                            tok = slice(P * t, P * t + P)
                            for k in range(KT):
                                last = split3(pe, ps[:, t, 0:RW], x_hi[:, k, tok], x_lo[:, k, tok],
                                              wf_hi[:, k, LW:FW], wf_lo[:, k, LW:FW], k == 0, k == KT - 1)
                            last.then_inc(right_mm, 1)
                        pe.wait_ge(base_added, at(b, 2 * NT, NT * f + 1))
                        pe.wait_ge(xaw_ready, at(b, 2, f + 1))
                        for t in range(NT):
                            last = pe.transpose(ps[:, 0, P * t:P * t + P], xa[:, t, :], ident2[:, :])
                        last.then_inc(xaT_mm, 1)
                        pe.wait_ge(xathi_ready, at(b, 2, f + 1))
                        pe.wait_ge(xatlo_ready, at(b, 2, f + 1))
                        pe.wait_ge(base_added, at(b, 2 * NT, NT * f + NT))
                        for t in range(NT):
                            tok = slice(P * t, P * t + P)
                            split3(pe, ps[:, 4 + t, :], xat_hi[:, tok], xat_lo[:, tok], lb_hi[:, :], lb_lo[:, :],
                                   True, True).then_inc(lora_mm, 1)

                    ffn(0)
                    turned(b, 1)
                    pe.wait_ge(xhi_ready, at(b, 3 * NT, 2 * NT))
                    pe.wait_ge(xlo_ready, at(b, 3 * NT, 2 * NT))
                    pe.wait_ge(ffn_added, at(b, 2 * NT, FFN_CREDIT + NT))
                    for n in range(NQ):
                        for k in range(KT):
                            last = split3(pe, ps[:, 4 + n, :], wq_hi[:, k, P * n:P * n + P], wq_lo[:, k, P * n:P * n + P],
                                          x_hi[:, k, :], x_lo[:, k, :], k == 0, k == KT - 1)
                        last.then_inc(q_mm, 1)
                    for n, done in ((0, k_mm), (1, v_mm)):
                        for k in range(KT):
                            last = split3(pe, ps[:, n, :], wkv_hi[:, k, DKV * n:DKV * n + DKV], wkv_lo[:, k, DKV * n:DKV * n + DKV],
                                          x_hi[:, k, :], x_lo[:, k, :], k == 0, k == KT - 1)
                        last.then_inc(done, 1)
                    pe.wait_ge(vT_ready, at(b, 1, 1))
                    for t in range(NT):
                        last = pe.transpose(ps[:, 2, P * t:P * t + P], vT[:, P * t:P * t + P], ident2[:, :])
                    last.then_inc(vtok_mm, 1)

                    def pick(m, hp, hi, lo, kind, done):
                        r = slice(2 * DH * hp, 2 * DH * hp + 2 * DH)
                        pe.matmul(ps[:, m % 4, :], sel[r, kind, :], hi[r, :], start=True, stop=False)
                        pe.matmul(ps[:, m % 4, :], sel[r, kind + 1, :], lo[r, :], start=False, stop=True).then_inc(done, 1)

                    pe.wait_ge(klo_ready, after(at(b, 1, 1)))
                    pe.wait_ge(khi_ready, at(b, 1, 1))
                    pe.wait_ge(v_ready, at(b, 1, 1))
                    for m in range(HP):
                        pick(m, m, k_hi, k_lo, 2, ksel_mm)
                    def pick_q(m):
                        if m < 4:
                            pe.wait_ge(kstack_ready, after(at(b, HP, m + 1)))
                        else:
                            pe.wait_ge(qstack_ready, after(at(b, NQ * HP, m - 3)))
                        if m % HP == 0:
                            pe.wait_ge(qlo_ready, at(b, NQ, m // HP + 1))
                        pick(m, m % HP, q_hi[:, m // HP, :], q_lo[:, m // HP, :], 0, qsel_mm)

                    for m in range(HP):
                        pick_q(m)
                    for t in range(NT):
                        if t == 0:
                            pe.wait_ge(qelu_ready, at(b, NQ, NQ))
                            pe.wait_ge(qlo_ready, at(b, NQ, NQ))
                        if t >= 2:
                            pe.wait_ge(amem_ready, at(b, NT, t - 1))
                        for n in range(NQ):
                            c0 = (DKV + 1) * (n % 2)
                            last = pe.matmul(ps[:, 4 + 2 * (t % 2) + n // 2, c0:c0 + DKV + 1], q_elu[:, n, P * t:P * t + P],
                                             mem_aug[:, :], start=True, stop=True)
                        last.then_inc(mem_mm, 1)
                    pe.wait_ge(amem_ready, at(b, NT, NT))
                    pe.wait_ge(v_ready, at(b, 1, 1))
                    def pair(h):
                        n, kv = divmod(h, NKV)
                        return n * HP + kv // 2, kv

                    for g in range(NH + OUT_LAG):
                        for j in range(2):
                            if 2 * g + j < (NQ - 1) * HP:
                                pick_q(HP + 2 * g + j)
                            if g < NH:
                                qt, kv = pair(g)
                                if g % 2 == 0 and j == 0:
                                    pe.wait_ge(qstack_ready, at(b, NQ * HP, qt + 1))
                                for st in (2 * j, 2 * j + 1):
                                    m = NT * g + st
                                    if m >= 2:
                                        pe.wait_ge(max_ready, at(b, NT * NH, m - 1))
                                    pe.matmul(ps[:, 4 + st % 2, :], q_stack[:, qt, P * st:P * st + P], k_stack[:, kv, :],
                                              start=True, stop=True).then_inc(max_mm, 1)
                            quad, i = divmod(g - 3, 4)
                            if i == 1 and j == 0 and 0 <= quad < QUADS:
                                pe.wait_ge(max_ready, at(b, NT * NH, 16 * quad + 16))
                                if quad:
                                    pe.wait_ge(shift_ready, at(b, QUADS, quad))
                                if turned_before(quad):
                                    pe.wait_ge(avn_ready, at(b, QUADS, turned_before(quad)))
                                for st in range(NT):
                                    last = pe.transpose(ps[0:4, 7, P * st:P * st + P], smax[:, 4 * quad:4 * quad + 4, st], ident2[:, :])
                                last.then_inc(maxT_mm, 1)
                            h = g - SCORE_LAG
                            if 0 <= h < NH:
                                qt, kv = pair(h)
                                if h == 0 and j == 0:
                                    pe.wait_ge(qstack_ready, at(b, NQ * HP, NQ * HP))
                                if h % 4 == 0 and j == 0:
                                    pe.wait_ge(shift_in, at(b, 64 * QUADS, 64 * (h // 4 + 1)))
                                for tt in (2 * j, 2 * j + 1):
                                    if tt % 2 == 0 and h:
                                        pe.wait_ge(exp_ready, at(b, 2 * NH, 2 * h + j - 1))
                                    last = pe.matmul(ps[:, tt, :], k_stack[:, kv, P * tt:P * tt + P], q_stack[:, qt, :],
                                                     start=True, stop=True)
                                last.then_inc(score_mm, 1)
                            quad, i = divmod(g - 3 - AV_LAG, 4)
                            if (i, j) in AV_SLOTS and 0 <= quad < QUADS:
                                tt = AV_SLOTS.index((i, j))
                                if tt == 0:
                                    pe.wait_ge(exp_ready, at(b, 2 * NH, 8 * quad + 8))
                                    if quad:
                                        pe.wait_ge(av_ready, at(b, QUADS, quad))
                                for e in range(4):
                                    h = 4 * quad + e
                                    last = pe.matmul(ps[32 * e:32 * e + 32, 6, :], v_aug[:, tt, h % NKV, :], probs[:, h % PROBS, tt, :],
                                                     start=tt == 0, stop=tt == NT - 1)
                                if tt == NT - 1:
                                    last.then_inc(av_mm, 1)
                        quad, i = divmod(g - 3 - TURN_LAG, 4)
                        if i == 0 and 0 <= quad < QUADS:
                            pe.wait_ge(av_ready, at(b, QUADS, quad + 1))
                            pe.wait_ge(shift_ready, at(b, QUADS, maxima_before(quad)))
                            if quad:
                                pe.wait_ge(avn_ready, at(b, QUADS, quad))
                            for t in range(NT):
                                last = pe.transpose(ps[:, 7, P * t:P * t + P], av_sb[:, quad % 2, P * t:P * t + P], ident2[:, :])
                            last.then_inc(avT_mm, 1)
                    turned(b, 2)
                    ffn(1)
                    turned(b, 3)

        @block.vector
        def _(dve):
            for n, (lo, hi, size) in enumerate(((wf_lo, wf_hi, KT * FW), (lb_lo, lb_hi, D), (wq_lo, wq_hi, KT * D),
                                                (wkv_lo, wkv_hi, KT * 2 * DKV))):
                dve.wait_ge(w_hi_done, n + 1)
                flat = (lambda a: a[:, :]) if n == 1 else (lambda a: a[:, :, :].rearrange("p k n -> p (k n)"))
                dve.tensor_tensor(flat(lo), stage[:, 0:size], flat(hi).bitcast(F32), ALU.subtract).then_inc(w_lo_done, 1)
            dve.sem_inc(ffn_added, FFN_CREDIT)
            dve.wait_ge(mem_tanh, 1)
            dve.tensor_scalar(mem_wc[:, :], mem_w[:, :], -0.5, 0.5, ALU.mult, ALU.add).then_inc(dve_consts, 1)
            dve.wait_ge(dve_consts, 1)
            dve.tensor_scalar(mem_w[:, :], mem_w[:, :], 0.5, 0.5, ALU.mult, ALU.add).then_inc(dve_consts, 1)
            dve.wait_ge(dve_consts, 2)
            dve.wait_ge(c_in, 112)
            dve.wait_ge(pool_consts, 3)
            dve.wait_ge(w_hi_done, 5)
            own = [0]

            def mark(ins):
                own[0] += 1
                ins.then_inc(dve_own, 1)

            def statistics(slot, t):
                mark(dve.bn_stats(stats[:, t, :], xs[:, slot, t, :]))

            def variances(b, f):
                for t in range(NT):
                    dve.wait_ge(dve_own, own[0] - NT + 1 + t)
                    dve.bn_aggr(mv[:, t, :], stats[:, t, :]).then_inc(var_ready, 1)

            def normalise(b, f, slot):
                dve.wait_ge(var_ready, at(b, 3 * NT, NT * (f + 1)))
                dve.wait_ge(rstd_ready, at(b, 3, f + 1))
                for t in range(NT):
                    dve.tensor_scalar(xn[:, t, :], xs[:, slot, t, :], mv[:, t, 0:1], rstd[:, t:t + 1],
                                      ALU.subtract, ALU.mult).then_inc(xn_ready, 1)

            def norm_lo(b, f):
                for t in range(NT):
                    dve.wait_ge(xhi_ready, at(b, 3 * NT, NT * f + t + 1))
                    dve.tensor_tensor(x_lo[:, :, P * t:P * t + P], ps[:, t, :].rearrange("p (k i) -> p k i", k=KT),
                                      x_hi[:, :, P * t:P * t + P].bitcast(F32), ALU.subtract).then_inc(xlo_ready, 1)

            dve.wait_ge(x_loaded[0], 16)
            for t in range(NT):
                statistics(0, t)
            variances(0, 0)
            normalise(0, 0, 0)
            norm_lo(0, 0)
            dve.wait_ge(dve_own, own[0])
            dve.sem_clear(dve_own)
            with dve.Fori(0, NBATCH // 2) as bb:
                for par in range(2):
                    b = bb * 2 + par
                    own[0] = 0

                    def ffn(f):
                        for t in range(NT):
                            dve.wait_ge(left_mm, at(b, 2 * NT, NT * f + t + 1))
                            dve.wait_ge(xa_ready, at(b, 4 * NT, 2 * NT * f + t + 1))
                            mark(dve.tensor_tensor(lg[:, t, :], ps[:, 4 + t, LW - NE:LW], gate_b_bc[:, :], ALU.add))
                        dve.wait_ge(dve_own, own[0])
                        mark(dve.tensor_reduce(lmax[:, :], lg[:, :, :], AX.X, ALU.max))
                        l_e = lg[:, :, :].rearrange("p t (e o) -> p t e o", o=1).to_broadcast([P, NT, NE, NE])
                        l_j = lg[:, :, :].rearrange("p t (o j) -> p t o j", o=1).to_broadcast([P, NT, NE, NE])
                        mark(dve.tensor_tensor(cmp_gt[:, :, :, :], l_j, l_e, ALU.is_gt))
                        mark(dve.tensor_tensor(cmp_eq[:, :, :, :], l_j, l_e, ALU.is_equal))
                        dve.wait_ge(dve_own, own[0] - 2)
                        dve.tensor_tensor(lp[:, :, :], lg[:, :, :],
                                          lmax[:, :].rearrange("p (t o) -> p t o", o=1).to_broadcast([P, NT, NE]),
                                          ALU.subtract).then_inc(ldiff_ready, 1)
                        dve.wait_ge(dve_own, own[0])
                        mark(dve.tensor_tensor(cmp_eq[:, :, :, :], cmp_eq[:, :, :, :],
                                               rank_mask[:, :, :].rearrange("p (o e) j -> p o e j", o=1).to_broadcast([P, NT, NE, NE]),
                                               ALU.mult))
                        dve.wait_ge(dve_own, own[0])
                        mark(dve.tensor_tensor(cmp_gt[:, :, :, :], cmp_gt[:, :, :, :], cmp_eq[:, :, :, :], ALU.add))
                        dve.wait_ge(dve_own, own[0])
                        mark(dve.tensor_reduce(rank[:, :], cmp_gt[:, :, :, :].rearrange("p t e j -> p (t e) j"), AX.X, ALU.add))
                        dve.wait_ge(dve_own, own[0])
                        dve.wait_ge(lp_ready, at(b, 2, f + 1))
                        lp2 = lp[:, :, :].rearrange("p t e -> p (t e)")
                        mark(dve.scalar_tensor_tensor(lp2, rank[:, :], 2.0, lp2, ALU.is_lt, ALU.mult))
                        dve.wait_ge(dve_own, own[0])
                        mark(dve.tensor_reduce(psum_g[:, :], lp[:, :, :], AX.X, ALU.add))
                        dve.wait_ge(dve_own, own[0])
                        mark(dve.reciprocal(psum_g[:, :], psum_g[:, :]))
                        dve.wait_ge(dve_own, own[0])
                        mark(dve.tensor_tensor(lp[:, :, :], lp[:, :, :],
                                               psum_g[:, :].rearrange("p (t o) -> p t o", o=1).to_broadcast([P, NT, NE]), ALU.mult))
                        dve.wait_ge(bias_added, at(b, 2 * NT, NT * (f + 1)))

                        def add_base(t):
                            dve.wait_ge(right_mm, at(b, 2 * NT, NT * f + t + 1))
                            dve.wait_ge(xa_ready, at(b, 4 * NT, 2 * NT * f + NT + t + 1))
                            for c, bank in ((0, 4 + t), (1, t)):
                                x2 = xs[:, par, t, D // 2 * c:D // 2 * c + D // 2]
                                last = dve.tensor_tensor(x2, x2, ps[:, bank, 0:D // 2], ALU.add)
                            last.then_inc(base_added, 1)

                        for t in range(NT - 1):
                            add_base(t)
                        dve.wait_ge(dve_own, own[0])
                        dve.wait_ge(xa_ready, at(b, 4 * NT, 2 * NT * (f + 1)))
                        xa3 = xa[:, :, :].rearrange("p t (e r) -> p (t e) r", e=NE)
                        dve.tensor_tensor(xa3, xa3, lp2.rearrange("p (e o) -> p e o", o=1).to_broadcast([P, NT * NE, RANK]),
                                          ALU.mult).then_inc(xaw_ready, 1)
                        add_base(NT - 1)
                        dve.wait_ge(xathi_ready, at(b, 2, f + 1))
                        dve.tensor_tensor(xat_lo[:, :], ps[:, 0, :], xat_hi[:, :].bitcast(F32), ALU.subtract).then_inc(xatlo_ready, 1)
                        if f == 1:
                            normalise(b, 3, 1 - par)
                        dve.wait_ge(base_added, at(b, 2 * NT, NT * (f + 1)))
                        for t in range(NT):
                            dve.wait_ge(lora_mm, at(b, 2 * NT, NT * f + t + 1))
                            dve.tensor_tensor(xs[:, par, t, :], xs[:, par, t, :], ps[:, 4 + t, :], ALU.add).then_inc(ffn_added, 1)
                            if f == 0:
                                dve.wait_ge(ffn_added, at(b, 2 * NT, FFN_CREDIT + t + 1))
                                statistics(par, t)

                    ffn(0)
                    variances(b, 1)
                    normalise(b, 1, par)
                    norm_lo(b, 1)
                    dve.wait_ge(khi_ready, at(b, 1, 1))
                    dve.tensor_tensor(k_lo[:, :], ps[:, 0, :], k_hi[:, :].bitcast(F32), ALU.subtract).then_inc(klo_ready, 1)
                    dve.wait_ge(vtok_mm, at(b, 1, 1))
                    dve.tensor_scalar(v_aug[:, :, :, 0:DH], ps[:, 2, :].rearrange("p (t h e) -> p t h e", t=NT, h=NKV),
                                      mem_wc[:, 0:1], None, ALU.mult).then_inc(v_ready, 1)
                    for n in range(NQ):
                        dve.wait_ge(qhi_ready, at(b, NQ, n + 1))
                        dve.wait_ge(qexp_ready, at(b, NQ, n + 1))
                        dve.tensor_tensor(q_lo[:, n, :], ps[:, 4 + n, :], q_hi[:, n, :].bitcast(F32), ALU.subtract).then_inc(qlo_ready, 1)
                    for m in range(HP):
                        dve.wait_ge(ksel_mm, at(b, HP, m + 1))
                        for e in range(2):
                            last = dve.tensor_scalar(k_stack[:, 2 * m + e, :], ps[:, m, :], head_rows[:, e, 0:1], head_rows[:, e, 1:2],
                                                     ALU.mult, ALU.add)
                        last.then_inc(kstack_ready, 1)
                    for n in range(NQ):
                        mark(dve.tensor_scalar(q_exp[:, n, :], q_exp[:, n, :], 1.0, -1.0, ALU.min, ALU.add))
                    for n in range(NQ):
                        dve.wait_ge(dve_own, own[0] - NQ + 1 + n)
                        dve.scalar_tensor_tensor(q_elu[:, n, :], ps[:, 4 + n, :], 0.0, q_exp[:, n, :], ALU.max, ALU.add).then_inc(qelu_ready, 1)
                    for t in range(NT):
                        dve.wait_ge(mem_mm, at(b, NT, t + 1))
                        pv = ps[:, 4 + 2 * (t % 2):6 + 2 * (t % 2), 0:2 * (DKV + 1)].rearrange("p c (n e) -> p c n e", n=2)
                        rc = mem_rc[:, t, :].rearrange("p (c n) -> p c n", c=2)
                        mark(dve.reciprocal(rc, pv[:, :, :, DKV]))
                        dve.wait_ge(dve_own, own[0])
                        mark(dve.tensor_scalar(rc, rc, mem_w[:, 0:1], None, ALU.mult))
                        dve.wait_ge(dve_own, own[0])
                        for c in range(2):
                            last = dve.tensor_tensor(a_mem[:, t, 2 * DKV * c:2 * DKV * c + 2 * DKV].rearrange("p (n e) -> p n e", n=2),
                                                     pv[:, c, :, 0:DKV],
                                                     rc[:, c, :].rearrange("p (n o) -> p n o", o=1).to_broadcast([P, 2, DKV]), ALU.mult)
                        last.then_inc(amem_ready, 1)
                    for g in range(NH + OUT_LAG):
                        quad, i = divmod(g - 3 - OUT_LAG, 4)
                        if i == 0 and 0 <= quad < QUADS:
                            dve.wait_ge(avT_mm, at(b, QUADS, quad + 1))
                            pv = ps[:, 7, :].rearrange("p (t h e) -> p t h e", t=NT, h=4)
                            mark(dve.reciprocal(av_rc[:, :, :], pv[:, :, :, DH]))
                            dve.wait_ge(dve_own, own[0])
                            if quad >= 2:
                                dve.wait_ge(adot_added, at(b, QUADS, quad - 1))
                            dve.tensor_tensor(av_n[:, quad % 2, :, :, :], pv[:, :, :, 0:DH],
                                              av_rc[:, :, :].rearrange("p t (h o) -> p t h o", o=1).to_broadcast([P, NT, 4, DH]),
                                              ALU.mult).then_inc(avn_ready, 1)
                        for st in range(NT):
                            if g < NH:
                                dve.wait_ge(max_mm, at(b, NT * NH, NT * g + st + 1))
                                dve.tensor_reduce(smax[:, g, st:st + 1], ps[:, 4 + st % 2, :], AX.X, ALU.max).then_inc(max_ready, 1)
                    dve.wait_ge(adot_added, at(b, QUADS, QUADS))
                    for t in range(NT):
                        statistics(par, t)
                    variances(b, 2)
                    normalise(b, 2, par)
                    norm_lo(b, 2)
                    dve.wait_ge(x_loaded[1 - par], bb * 16 + (16 if par == 0 else 32))
                    for t in range(NT):
                        statistics(1 - par, t)
                    variances(b, 3)
                    ffn(1)
                    norm_lo(b, 3)
                    dve.wait_ge(dve_own, own[0])
                    dve.sem_clear(dve_own)


def kernel(L0_attn_a_x, L0_attn_a_Wq, L0_attn_a_Wk, L0_attn_a_Wv, L0_attn_a_Wbeta, L0_attn_a_Wg1, L0_attn_a_Wg2, L0_attn_a_g_norm,
           L0_attn_a_Wo, L0_attn_b_Wq, L0_attn_b_Wk, L0_attn_b_Wv, L0_attn_b_memory, L0_attn_b_memory_norm, L0_attn_b_memory_weight,
           L0_ffn_W, L0_ffn_b, L0_ffn_lora_A, L0_ffn_lora_B, L0_ffn_gate_w, L0_ffn_gate_b):
    import numpy as np
    import concourse.bacc as bacc
    from concourse.bass_utils import run_bass_kernel_spmd

    def by_input(w):
        w = np.asarray(w)
        o, d = w.shape
        return np.ascontiguousarray(w.T.reshape(d // P, P, o).transpose(1, 0, 2).reshape(P, -1))

    def on_all(v):
        v = np.asarray(v).reshape(1, -1)
        return np.ascontiguousarray(np.broadcast_to(v, (P, v.shape[1])))

    j = np.arange(C)
    causal = np.concatenate([j[:, None] < j[None, :], j[:, None] <= j[None, :]], 1).astype(np.float32)
    e = np.arange(NE)
    sel = np.zeros((4, 2, DH, 2, 4, DH), np.float32)
    for kind, parts in enumerate(((0, 2), (1,), (0, 1), (2,))):
        for part in parts:
            sel[kind, :, :, :, part] = np.eye(2 * DH, dtype=np.float32).reshape(2, DH, 2, DH)
    sel = np.tile(sel.reshape(4, 2 * DH, P).transpose(1, 0, 2).reshape(2 * DH, 4 * P), (P // (2 * DH), 1))
    row = np.arange(P)
    head_rows = np.stack([np.stack([row // 64 == e, row == 64 * e + 3 * DH], 1) for e in range(2)], 1).astype(np.float32).reshape(P, 4)
    x = np.ascontiguousarray(np.asarray(L0_attn_a_x))
    w_f, lora_a, gate_w = np.asarray(L0_ffn_W), np.asarray(L0_ffn_lora_A).reshape(ER, D), np.asarray(L0_ffn_gate_w)
    arrays = {
        "in_x": x,
        "in_w_main": np.stack([by_input(w) for w in (L0_attn_a_Wk, L0_attn_a_Wq, L0_attn_a_Wv, L0_attn_a_Wo)]),
        "in_w_gb": by_input(np.concatenate([np.asarray(L0_attn_a_Wg1), np.asarray(L0_attn_a_Wbeta)], 0)),
        "in_w_g2": np.ascontiguousarray(np.asarray(L0_attn_a_Wg2).T),
        "in_g_norm": np.ascontiguousarray(np.asarray(L0_attn_a_g_norm).reshape(KT, P).T),
        "in_ident": np.eye(P, dtype=np.float32),
        "in_masks": np.concatenate([causal, causal], 0),
        "in_head_ones": np.kron(np.eye(HPT), np.ones((HD, HD))).astype(np.float32),
        "in_w_ffn": by_input(np.concatenate([w_f[:D // 2], lora_a[:ER // 2], gate_w, w_f[D // 2:], lora_a[ER // 2:]], 0)),
        "in_b_ffn": on_all(L0_ffn_b),
        "in_lora_b": np.ascontiguousarray(np.asarray(L0_ffn_lora_B).transpose(0, 2, 1).reshape(ER, D)),
        "in_gate_b": on_all(L0_ffn_gate_b),
        "in_w_q": by_input(L0_attn_b_Wq),
        "in_w_kv": by_input(np.concatenate([np.asarray(L0_attn_b_Wk), np.asarray(L0_attn_b_Wv)], 0)),
        "in_mem_aug": np.concatenate([np.asarray(L0_attn_b_memory), np.asarray(L0_attn_b_memory_norm)], 1),
        "in_mem_w": on_all(L0_attn_b_memory_weight),
        "in_sel": sel,
        "in_head_rows": head_rows,
        "in_rank_mask": on_all(e[None, :] < e[:, None]).astype(np.float32),
    }
    arrays = {k: np.ascontiguousarray(v) for k, v in arrays.items()}

    nc = bacc.Bacc("TRN2", target_bir_lowering=False, num_devices=1)
    a = {k: nc.dram_tensor(k, v.shape, mybir.dt.from_np(v.dtype), kind="ExternalInput").ap() for k, v in arrays.items()}
    out = nc.dram_tensor("y", x.shape, F32, kind="ExternalOutput").ap()
    x2 = nc.dram_tensor("x2", x.shape, F32, kind="Internal").ap()
    dims = x.shape[:2]
    delta_rule_layer(nc, dims, a["in_x"], a["in_w_main"], a["in_w_gb"], a["in_w_g2"], a["in_g_norm"], a["in_ident"],
                     a["in_masks"], a["in_head_ones"], x2)
    token_layers(nc, dims, x2, a["in_w_ffn"], a["in_b_ffn"], a["in_lora_b"], a["in_gate_b"], a["in_w_q"], a["in_w_kv"],
                 a["in_mem_aug"], a["in_mem_w"], a["in_ident"], a["in_rank_mask"], a["in_sel"], a["in_head_rows"], out)
    r = run_bass_kernel_spmd(nc, [arrays], core_ids=[0])
    return r.results[0]["y"]
```
